# Optimizing a Trainium2 kernel written in Bass

```python
import numpy as np
import jax
import jax.numpy as jnp

def _softmax(x, axis=-1):
    return jax.nn.softmax(x, axis=axis)

def _gelu(x):
    return jax.nn.gelu(x, approximate=True)

def _silu(x):
    return jax.nn.silu(x)

def _sigmoid(x):
    return jax.nn.sigmoid(x)

def _layernorm(x, axis=-1, eps=1e-05):
    m = jnp.mean(x, axis=axis, keepdims=True)
    v = jnp.var(x, axis=axis, keepdims=True)
    return (x - m) / jnp.sqrt(v + eps)

def _scatter_add(tgt, idx, src, axis=0):
    return tgt.at[idx].add(src)

def _segment_sum(src, seg, n):
    return jax.ops.segment_sum(src, seg, n)
kernel_name = 'mk_metaformer_d1_conv_nchw128_r2_5d9802'

def setup_inputs(seed: int=0):
    np.random.seed(seed)
    _w = jnp.asarray

    def _rec_inputs():
        import jax
        import jax.numpy as jnp
        _gk = jax.random.key(seed)
        x = -0.0005207 + 1.001 * jax.random.normal(jax.random.fold_in(_gk, 1), (4, 64, 32, 32), jnp.float32)
        return x
    x = _rec_inputs()

    def _L0_conv_setup():
        import jax, jax.numpy as jnp
        import numpy as np
        KS, STRIDE, PAD, GROUPS = (7, 1, 3, 8)

        def _patches(a, fH, fW):
            cols = []
            for ki in range(KS):
                rows = []
                for kj in range(KS):
                    rows.append(a[:, :, ki:ki + (fH - 1) * STRIDE + 1:STRIDE, kj:kj + (fW - 1) * STRIDE + 1:STRIDE])
                cols.append(jnp.stack(rows, axis=-1))
            return jnp.stack(cols, axis=-2)
        key = jax.random.key(seed)
        ks = jax.random.split(key, 6)
        B, C, H, W = (4, 64, 32, 32)
        O = 64
        rel_size = O // GROUPS // 2
        return {'x': jax.random.normal(ks[0], (B, C, H, W), jnp.float32), 'wq': jax.random.normal(ks[1], (O, C), jnp.float32) * 0.05, 'wk': jax.random.normal(ks[2], (O, C), jnp.float32) * 0.05, 'wv': jax.random.normal(ks[3], (O, C), jnp.float32) * 0.05, 'rel_x': jax.random.normal(ks[4], (rel_size, KS), jnp.float32), 'rel_y': jax.random.normal(ks[5], (O // GROUPS - rel_size, KS), jnp.float32)}
    _L0_conv_all = _L0_conv_setup()
    _L0_conv_in = {k: v for k, v in _L0_conv_all.items() if k in ('wq', 'wk', 'wv', 'rel_x', 'rel_y')}
    del _L0_conv_all

    def _L0_ffn_setup():
        import jax, jax.numpy as jnp
        import numpy as np
        NB, NOPS = (33, 19)
        D, H = (64, 256)
        B, S = (8, 512)
        CARRY_OPS = [0, 1, 2, 10, 11, 12, 13]

        def _build_masks():
            am = np.zeros((NB, NOPS), dtype=bool)
            fm = np.zeros((NB, NOPS), dtype=bool)
            fm[0, :] = True
            for b in range(1, 8):
                am[b, CARRY_OPS] = True
                fm[b, CARRY_OPS] = True
            am[8, [14, 15, 8, 9]] = True
            fm[8, [14, 15, 8, 9]] = True
            for b in range(16, 32):
                fm[b, [3, 4]] = True
            am[32, [10, 11, 12, 13]] = True
            fm[32, [5, 6, 7, 2, 4, 10, 11, 12, 13]] = True
            return (jnp.asarray(am), jnp.asarray(fm))
        key = jax.random.key(seed)
        ks = jax.random.split(key, 9)
        sd = 1.0 / np.sqrt(D)
        sh = 1.0 / np.sqrt(H)
        am, fm = _build_masks()
        return {'x': jax.random.normal(ks[0], (B, S, D), jnp.float32), 'ffn_w1': jax.random.normal(ks[1], (NB, NOPS, D, H), jnp.float32) * sd, 'ffn_b1': jnp.zeros((NB, NOPS, H), jnp.float32), 'ffn_w2': jax.random.normal(ks[2], (NB, NOPS, H, D), jnp.float32) * sh, 'ffn_b2': jnp.zeros((NB, NOPS, D), jnp.float32), 'wq': jax.random.normal(ks[3], (NB, NOPS, D, D), jnp.float32) * sd, 'wk': jax.random.normal(ks[4], (NB, NOPS, D, D), jnp.float32) * sd, 'wv': jax.random.normal(ks[5], (NB, NOPS, D, D), jnp.float32) * sd, 'wo': jax.random.normal(ks[6], (NB, NOPS, D, D), jnp.float32) * sd, 'attn_mask': am, 'ffn_mask': fm}
    _L0_ffn_all = _L0_ffn_setup()
    _L0_ffn_in = {k: v for k, v in _L0_ffn_all.items() if k in ('ffn_w1', 'ffn_b1', 'ffn_w2', 'ffn_b2', 'wq', 'wk', 'wv', 'wo', 'attn_mask', 'ffn_mask')}
    del _L0_ffn_all
    return {'x': x, 'L0_conv_wq': _L0_conv_in['wq'], 'L0_conv_wk': _L0_conv_in['wk'], 'L0_conv_wv': _L0_conv_in['wv'], 'L0_conv_rel_x': _L0_conv_in['rel_x'], 'L0_conv_rel_y': _L0_conv_in['rel_y'], 'L0_ffn_ffn_w1': _L0_ffn_in['ffn_w1'], 'L0_ffn_ffn_b1': _L0_ffn_in['ffn_b1'], 'L0_ffn_ffn_w2': _L0_ffn_in['ffn_w2'], 'L0_ffn_ffn_b2': _L0_ffn_in['ffn_b2'], 'L0_ffn_wq': _L0_ffn_in['wq'], 'L0_ffn_wk': _L0_ffn_in['wk'], 'L0_ffn_wv': _L0_ffn_in['wv'], 'L0_ffn_wo': _L0_ffn_in['wo'], 'L0_ffn_attn_mask': _L0_ffn_in['attn_mask'], 'L0_ffn_ffn_mask': _L0_ffn_in['ffn_mask']}

def reference(x, L0_conv_wq, L0_conv_wk, L0_conv_wv, L0_conv_rel_x, L0_conv_rel_y, L0_ffn_ffn_w1, L0_ffn_ffn_b1, L0_ffn_ffn_w2, L0_ffn_ffn_b2, L0_ffn_wq, L0_ffn_wk, L0_ffn_wv, L0_ffn_wo, L0_ffn_attn_mask, L0_ffn_ffn_mask):
    import jax
    import jax.numpy as jnp

    def _L0_conv_ref(x, wq, wk, wv, rel_x, rel_y):
        import jax, jax.numpy as jnp
        import numpy as np
        KS, STRIDE, PAD, GROUPS = (7, 1, 3, 8)

        def _patches(a, fH, fW):
            cols = []
            for ki in range(KS):
                rows = []
                for kj in range(KS):
                    rows.append(a[:, :, ki:ki + (fH - 1) * STRIDE + 1:STRIDE, kj:kj + (fW - 1) * STRIDE + 1:STRIDE])
                cols.append(jnp.stack(rows, axis=-1))
            return jnp.stack(cols, axis=-2)
        B, C, H, W = x.shape
        O = wq.shape[0]
        rel_size = rel_x.shape[0]
        xp = jnp.pad(x, ((0, 0), (0, 0), (PAD, PAD), (PAD, PAD)))
        pH, pW = (H + 2 * PAD, W + 2 * PAD)
        fH, fW = ((pH - KS) // STRIDE + 1, (pW - KS) // STRIDE + 1)
        q = jnp.einsum('oc,bchw->bohw', wq, xp)
        k = jnp.einsum('oc,bchw->bohw', wk, xp)
        v = jnp.einsum('oc,bchw->bohw', wv, xp)
        h0 = (KS - 1) // 2
        win_q = q[:, :, h0:pH - KS // 2:STRIDE, h0:pW - KS // 2:STRIDE]
        win_q_b = win_q.reshape(B, GROUPS, O // GROUPS, fH, fW)
        qx = win_q_b[:, :, :rel_size]
        qy = win_q_b[:, :, rel_size:]
        bias_x = jnp.einsum('bgxhw,xk->bhwk', qx, rel_x)
        bias_y = jnp.einsum('bgyhw,yk->bhwk', qy, rel_y)
        win_k = _patches(k, fH, fW)
        win_v = _patches(v, fH, fW)
        logits = jnp.einsum('bchw,bchwkl->bhwkl', win_q, win_k)
        logits = logits + bias_x[:, :, :, None, :] + bias_y[:, :, :, :, None]
        attn = jax.nn.softmax(logits.reshape(B, fH, fW, KS * KS), axis=-1)
        attn = attn.reshape(B, fH, fW, KS, KS)
        out = jnp.einsum('bhwkl,bchwkl->bchw', attn, win_v)
        return out

    def _L0_ffn_ref(x, ffn_w1, ffn_b1, ffn_w2, ffn_b2, wq, wk, wv, wo, attn_mask, ffn_mask):
        import jax, jax.numpy as jnp
        import numpy as np
        NB, NOPS = (33, 19)
        D, H = (64, 256)
        B, S = (8, 512)
        CARRY_OPS = [0, 1, 2, 10, 11, 12, 13]

        def _build_masks():
            am = np.zeros((NB, NOPS), dtype=bool)
            fm = np.zeros((NB, NOPS), dtype=bool)
            fm[0, :] = True
            for b in range(1, 8):
                am[b, CARRY_OPS] = True
                fm[b, CARRY_OPS] = True
            am[8, [14, 15, 8, 9]] = True
            fm[8, [14, 15, 8, 9]] = True
            for b in range(16, 32):
                fm[b, [3, 4]] = True
            am[32, [10, 11, 12, 13]] = True
            fm[32, [5, 6, 7, 2, 4, 10, 11, 12, 13]] = True
            return (jnp.asarray(am), jnp.asarray(fm))
        scale = jnp.asarray(1.0 / np.sqrt(D), x.dtype)

        def step(h, p):
            op = jnp.argmax(h[0, 0, :NOPS])
            q = h @ p['wq'][op]
            k = h @ p['wk'][op]
            v = h @ p['wv'][op]
            attn = jax.nn.softmax(jnp.einsum('bqd,bkd->bqk', q, k) * scale, axis=-1)
            y = jnp.einsum('bqk,bkd->bqd', attn, v) @ p['wo'][op]
            h = jnp.where(p['am'][op], y, h)
            z = jax.nn.relu(h @ p['w1'][op] + p['b1'][op]) @ p['w2'][op] + p['b2'][op]
            h = jnp.where(p['fm'][op], z, h)
            return (h, None)
        xs = {'w1': ffn_w1, 'b1': ffn_b1, 'w2': ffn_w2, 'b2': ffn_b2, 'wq': wq, 'wk': wk, 'wv': wv, 'wo': wo, 'am': attn_mask, 'fm': ffn_mask}
        out, _ = jax.lax.scan(step, x, xs)
        return out

    def _gn(v, G=32, eps=1e-05):
        B_, C_, H_, W_ = v.shape
        g = v.reshape(B_, G, C_ // G, H_, W_)
        m = jnp.mean(g, axis=(2, 3, 4), keepdims=True)
        s = jnp.var(g, axis=(2, 3, 4), keepdims=True)
        return ((g - m) / jnp.sqrt(s + eps)).reshape(v.shape)

    def _ln_c(v, eps=1e-06):
        m = jnp.mean(v, axis=1, keepdims=True)
        s = jnp.var(v, axis=1, keepdims=True)
        return (v - m) / jnp.sqrt(s + eps)

    def _ln_t(v, eps=1e-05):
        m = jnp.mean(v, axis=-1, keepdims=True)
        s = jnp.var(v, axis=-1, keepdims=True)
        return (v - m) / jnp.sqrt(s + eps)

    def _to_tokens(v):
        B_, C_, H_, W_ = v.shape
        return v.reshape(B_, C_, H_ * W_).transpose(0, 2, 1)

    def _from_tokens(t, like):
        B_, C_, H_, W_ = like.shape
        return t.transpose(0, 2, 1).reshape(B_, C_, H_, W_)
    x = x + _L0_conv_ref(_ln_c(x), L0_conv_wq, L0_conv_wk, L0_conv_wv, L0_conv_rel_x, L0_conv_rel_y)
    t = _to_tokens(x)
    t = t + _L0_ffn_ref(_ln_t(t), L0_ffn_ffn_w1, L0_ffn_ffn_b1, L0_ffn_ffn_w2, L0_ffn_ffn_b2, L0_ffn_wq, L0_ffn_wk, L0_ffn_wv, L0_ffn_wo, L0_ffn_attn_mask, L0_ffn_ffn_mask)
    x = _from_tokens(t, x)
    return x

_drawn_inputs = setup_inputs


def setup_inputs(seed=0):
    import zlib

    import numpy as np

    out = dict(_drawn_inputs(seed))
    spreads = {'L0_ffn_ffn_b1': (0.0, 0.1), 'L0_ffn_ffn_b2': (0.0, 0.1)}
    factors = {'L0_ffn_wq': 4.493, 'L0_ffn_wk': 5.575}
    for name, (base, spread) in spreads.items():
        noise = np.random.default_rng([zlib.crc32(name.encode()), seed]).standard_normal(out[name].shape)
        drawn = base * np.exp(spread * noise) if base else spread * noise
        out[name] = jnp.asarray(drawn.astype(out[name].dtype))
    for name, factor in factors.items():
        out[name] = (out[name] * factor).astype(out[name].dtype)
    return out
```

```python
from contextlib import ExitStack

import concourse.bass as bass
from concourse import mybir

F32 = mybir.dt.float32
I32 = mybir.dt.int32
U32 = mybir.dt.uint32
U8 = mybir.dt.uint8
ALU = mybir.AluOpType
ACT = mybir.ActivationFunctionType
X = mybir.AxisListType.X

P = 128
C = 64
HH, WW = 32, 32
NPOS = HH * WW
COLS = 2 * NPOS
KS, PAD = 7, 3
HP, WP = HH + 2 * PAD, WW + 2 * PAD
BR, BC = 8, 16
KR, KC = BR + KS - 1, BC + KS - 1
NKEY = KR * KC
NCH, CH = 3, 103
NPAIR = 16
XROW, YROW = 64, 96
TX, TY = 32 + KC - 1, 32 + KR - 1
NB, NOPS, HID = 33, 19, 256
NTILE = 16
NKC = NPOS // P
SCALE = float(C) ** -0.5
LN_C_EPS, LN_T_EPS = 1e-6, 1e-5
W2COLS = 2 * C + 2 + 1


def build(nc, x, w_qk, w_q, w_v, bias_tables, key_onehot, masks, ident, mean_mat, iotas,
          attn_mask, ffn_mask, attn_pack, ffn_w1, ffn_pack, out):
    with ExitStack() as ctx:
        def sb(name, shape, dt=F32):
            return ctx.enter_context(nc.sbuf_tensor(name, shape, dt))

        def sem(name):
            return ctx.enter_context(nc.semaphore(name))

        ps = ctx.enter_context(nc.psum_tensor("ps", [P, 8, 512], F32))

        eye = sb("eye", [P, P])
        mean_w = sb("mean_w", [P, P])
        mask_x = sb("mask_x", [P, WW + HH])
        wqk = sb("wqk", [P, 2, P])
        wq_nat = sb("wq_nat", [C, C])
        wv_bd = sb("wv_bd", [P, P])
        rel_tab = sb("rel_tab", [C, TX + TY])
        gx = sb("gx", [P, KC, 2, 32])
        gy = sb("gy", [P, KR, 2, 32])
        eps_c = sb("eps_c", [P, 2])
        ones_c = sb("ones_c", [P, 1])
        x2 = sb("x2", [P, 2, HH, WW])
        xc = sb("xc", [P, COLS])
        sq = sb("sq", [P, COLS])
        h2 = sb("h2", [P, COLS])
        q_aug = sb("q_aug", [P, 4, HH, WW])
        k_aug = sb("k_aug", [P, 4, HP, WP])
        v_pad = sb("v_pad", [P, 2, HP, WP])
        q_st = sb("q_st", [P, 2, 2, BR * BC])
        v_st = sb("v_st", [P, 2, NCH * CH])
        v_key = sb("v_key", [P, 2, NCH, P])
        prob = sb("prob", [P, 2, 2, NCH * CH])
        prob_t = sb("prob_t", [P, 2, 2, NCH, P])
        negmax = sb("negmax", [P, 2, 2])
        rowsum = sb("rowsum", [P, 2, 2])
        rinv = sb("rinv", [P, 2, 2])
        row = sb("row", [1, C])
        masks8 = sb("masks8", [1, 2, NB * NOPS], U8)
        kinds = sb("kinds", [1, NB, NOPS])
        fm_f = sb("fm_f", [1, NB * NOPS])
        iota = sb("iota", [1, NOPS + 2 * NB])
        top8 = sb("top8", [1, 8])
        idx8 = sb("idx8", [1, 8], U32)
        onehot = sb("onehot", [1, NOPS])
        picked = sb("picked", [1, NB, NOPS])
        sc = sb("sc", [1, 16])
        rw = sb("rw", [1, 4, NB])
        info = sb("info", [1, 4], I32)
        wa = sb("wa", [C, 4, C])
        qk_bd = sb("qk_bd", [P, P])
        vo_bd = sb("vo_bd", [P, P])
        g_half = sb("g_half", [P, 2, NPOS])
        pr = q_aug[:, 0:2].rearrange("p a h w -> p a (h w)")
        hs = q_aug[:, 2].rearrange("p h w -> p (h w)")
        vk = q_aug[:, 3].rearrange("p (k e) w -> p k (e w)", k=NKC)
        prt = sb("prt", [P, 2, 2, NKC, 512])
        wT = sb("wT", [C, 3, C])
        w1z = sb("w1z", [P, 2, HID])
        w2p = sb("w2p", [P, W2COLS])
        hid = xc.rearrange("p (a b) -> p a b", a=4)
        hid2 = sq.rearrange("p (a b) -> p a b", a=4)

        names = """x_loaded w_loaded c_loaded zeroed w_zeroed eps_set
            mean_ready centered squared var_ready std_ready rstd_ready normed
            tab_ready tab_copied qk_ready q_copied k_copied v_ready v_copied bias_ready bias_added
            q_staged v_staged scores_ready negmax_ready exp_done rinv_ready probs_ready
            probs_turned pt_copied v_turned vk_copied pv_done mixed
            row_turned dve_step decided passed info_read section_done
            aw_loaded fw_loaded w_turned wt_copied fold_ready fold_a fold_d
            h_staged g_ready g_act g_dve vo_ready vo_act vo_dve
            s_ready s_negmax s_exp s_rinv s_prob s_turned s_pta s_ptd s_pv
            hid_ready relu_act relu_dve hid_down z_ready
            out_ready stored""".split()
        S = {n: sem(n) for n in names}

        x_half = [x[2 * h:2 * h + 2].rearrange("b c r w -> c b r w") for h in range(2)]
        o_half = [out[2 * h:2 * h + 2].rearrange("b c r w -> c b (r w)") for h in range(2)]
        x2f = x2.rearrange("p a h w -> p (a h w)")

        block = ctx.enter_context(nc.Block())

        def load_info(eng, regs, n):
            eng.wait_ge(S["decided"], n)
            eng.sem_inc(S["passed"], 1)
            eng.load(regs, info[0:1, 0:4])
            eng.sem_inc(S["info_read"], 1)

        def routed(eng, attention, feed_forward, decide=None):
            regs = [eng.alloc_register(f"{eng.engine.name}_info{k}") for k in range(4)]
            n_att = eng.alloc_register(f"{eng.engine.name}_n_att")
            n_ffn = eng.alloc_register(f"{eng.engine.name}_n_ffn")
            eng.reg_mov(n_att, 0)
            eng.reg_mov(n_ffn, 0)
            load_info(eng, regs, 1)
            with eng.Fori(0, NB) as e:
                step = eng.snap(regs[0], min_val=0, max_val=NB)
                with eng.If(step < NB):
                    wrow = eng.snap(regs[1], min_val=0, max_val=NB * NOPS - 1)
                    am = eng.snap(regs[2], min_val=0, max_val=1)
                    with eng.If(am > 0):
                        a = eng.snap(n_att, min_val=0, max_val=NB - 1)
                        f = eng.snap(n_ffn, min_val=0, max_val=NB - 1)
                        attention(a, f, wrow)
                        eng.reg_add(n_att, n_att, 1)
                    with eng.Else():
                        eng.nop()
                    fm = eng.snap(regs[3], min_val=0, max_val=1)
                    with eng.If(fm > 0):
                        a = eng.snap(n_att, min_val=0, max_val=NB)
                        f = eng.snap(n_ffn, min_val=0, max_val=NB - 1)
                        feed_forward(a, f, wrow)
                        eng.reg_add(n_ffn, n_ffn, 1)
                    with eng.Else():
                        eng.nop()
                    if decide is not None:
                        a = eng.snap(n_att, min_val=0, max_val=NB)
                        f = eng.snap(n_ffn, min_val=0, max_val=NB)
                        decide(a, f, e + 1)
                    load_info(eng, regs, e + 2)
                with eng.Else():
                    eng.nop()
            return n_att, n_ffn

        @block.sync
        def _(sp):
            for h in range(2):
                sp.dma_start(x2[C * h:C * h + C], x_half[h]).then_inc(S["x_loaded"], 16)
            sp.dma_start(mean_w[:], mean_mat).then_inc(S["x_loaded"], 16)
            sp.wait_ge(S["w_zeroed"], 1)
            for h in range(2):
                sp.dma_start(wqk[C * h:C * h + C, h, :], w_qk).then_inc(S["w_loaded"], 16)
                sp.dma_start(wv_bd[C * h:C * h + C, C * h:C * h + C], w_v).then_inc(S["w_loaded"], 16)
            sp.dma_start(wq_nat[:], w_q).then_inc(S["w_loaded"], 16)
            sp.dma_start(rel_tab[:], bias_tables).then_inc(S["w_loaded"], 16)
            sp.dma_start(eye[:], ident).then_inc(S["c_loaded"], 16)
            sp.dma_start(mask_x[:], masks).then_inc(S["c_loaded"], 16)
            for b in range(4):
                sp.dma_start(k_aug[C:P, b, :, :], key_onehot).then_inc(S["c_loaded"], 16)
            sp.dma_start(iota[:], iotas).then_inc(S["c_loaded"], 16)
            sp.dma_start(masks8[:, 0, :], attn_mask).then_inc(S["c_loaded"], 16)
            sp.dma_start(masks8[:, 1, :], ffn_mask).then_inc(S["c_loaded"], 16)

            def attention(a, f, wrow):
                sp.dma_start(wa[:], attn_pack[bass.ds(wrow, 1)].rearrange("o c k d -> (o c) k d")
                             ).then_inc(S["aw_loaded"], 16)

            def feed_forward(a, f, wrow):
                for h in range(2):
                    sp.dma_start(w1z[C * h:C * h + C, h, :],
                                 ffn_w1[bass.ds(wrow, 1)].rearrange("o c k -> (o c) k")
                                 ).then_inc(S["fw_loaded"], 16)
                sp.dma_start(w2p[:], ffn_pack[bass.ds(wrow, 1)].rearrange("o p k -> (o p) k")
                             ).then_inc(S["fw_loaded"], 16)

            routed(sp, attention, feed_forward)
            for j in range(4):
                sp.wait_ge(S["out_ready"], j + 1)
                for h in range(2):
                    sp.dma_start(o_half[h][:, j // 2, (j % 2) * 512:(j % 2) * 512 + 512],
                                 xc[C * h:C * h + C, j * 512:j * 512 + 512]).then_inc(S["stored"], 16)
            sp.wait_ge(S["stored"], 16 * 8)

        @block.gpsimd
        def _(pool):
            nc.gpsimd.memset(ones_c[:], 1.0)
            nc.gpsimd.memset(wqk[:], 0.0)
            nc.gpsimd.memset(wv_bd[:], 0.0).then_inc(S["w_zeroed"], 1)
            nc.gpsimd.memset(gx[:], 0.0)
            nc.gpsimd.memset(gy[:], 0.0)
            nc.gpsimd.memset(k_aug[0:C], 0.0)
            nc.gpsimd.memset(v_pad[:], 0.0)
            nc.gpsimd.memset(v_st[:], 0.0)
            nc.gpsimd.memset(prob[:], 0.0)
            nc.gpsimd.memset(qk_bd[:], 0.0)
            nc.gpsimd.memset(vo_bd[:], 0.0)
            nc.gpsimd.memset(g_half[:], 0.0)
            nc.gpsimd.memset(w1z[:], 0.0).then_inc(S["zeroed"], 1)

            def stage(b2, hb, xb, p, early=False):
                if early:
                    if xb == 0:
                        pool.wait_ge(S["q_copied"], 8)
                        pool.wait_ge(S["bias_added"], 16)
                        pool.wait_ge(S["v_copied"], 4)
                else:
                    pool.wait_ge(S["scores_ready"], p - 1)
                for h in range(2):
                    src = q_aug[:, bass.ds(2 * h + b2, 1), bass.ds(BR * hb, BR), BC * xb:BC * xb + BC]
                    ins = nc.gpsimd.tensor_tensor(
                        q_st[:, xb, h, :].rearrange("p (a r c) -> p a r c", a=1, c=BC), src,
                        ones_c[:].unsqueeze(2).unsqueeze(3).broadcast_to([P, 1, BR, BC]), ALU.mult)
                ins.then_inc(S["q_staged"], 1)
                if not early:
                    pool.wait_ge(S["v_turned"], p - 1)
                src = v_pad[:, bass.ds(b2, 1), bass.ds(BR * hb, KR), BC * xb:BC * xb + KC]
                nc.gpsimd.tensor_tensor(
                    v_st[:, xb, 0:NKEY].rearrange("p (a r c) -> p a r c", a=1, c=KC), src,
                    ones_c[:].unsqueeze(2).unsqueeze(3).broadcast_to([P, 1, KR, KC]), ALU.mult
                    ).then_inc(S["v_staged"], 1)

            for xb in range(2):
                stage(0, 0, xb, xb, early=True)
            with pool.Fori(1, 8) as r:
                b2 = pool.snap(r // 4)
                hb = pool.snap(r % 4)
                for xb in range(2):
                    stage(b2, hb, xb, 2 * r + xb)

            routed(pool, lambda a, f, wrow: pool.nop(), lambda a, f, wrow: pool.nop())

        @block.tensor
        def _(pe):
            def norm(src, k):
                for j in range(4):
                    nc.tensor.matmul(ps[:, j, :], mean_w[:], src[:, j * 512:j * 512 + 512],
                                     start=True, stop=True).then_inc(S["mean_ready"], 1)
                for j in range(4):
                    pe.wait_ge(S["squared"], 4 * k + j + 1)
                    nc.tensor.matmul(ps[:, 4 + j, :], mean_w[:], sq[:, j * 512:j * 512 + 512],
                                     start=True, stop=True).then_inc(S["var_ready"], 1)

            pe.wait_ge(S["x_loaded"], 48)
            norm(x2f, 0)

            pe.wait_ge(S["w_loaded"], 96)
            for h in range(2):
                mm = nc.tensor.matmul(ps[C * h:C * h + C, 0, 0:TX + TY], wq_nat[:], rel_tab[:],
                                      start=True, stop=True)
            mm.then_inc(S["tab_ready"], 1)
            pe.wait_ge(S["tab_copied"], 4)
            for j in range(4):
                pe.wait_ge(S["normed"], 4 if j == 3 else max(j + 1, 2))
                if j == 2:
                    pe.wait_ge(S["rstd_ready"], 4)
                for h in range(2):
                    nc.tensor.matmul(ps[:, 2 * j + h, :], wqk[:, h, :], h2[:, j * 512:j * 512 + 512],
                                     start=True, stop=True).then_inc(S["qk_ready"], 1)
            pe.wait_ge(S["q_copied"], 4)
            pe.wait_ge(S["k_copied"], 4)
            for j in range(4):
                nc.tensor.matmul(ps[:, j, :], wv_bd[:], h2[:, j * 512:j * 512 + 512],
                                 start=True, stop=True).then_inc(S["v_ready"], 1)
            h4 = h2.rearrange("p (a h w) -> p a h w", a=2, w=WW)
            pe.wait_ge(S["q_copied"], 8)
            pe.wait_ge(S["k_copied"], 8)
            for w in range(WW):
                s0 = (-w) % KC
                mm = nc.tensor.matmul(ps[0:C, 4 + w // 8, (w % 8) * 64:(w % 8) * 64 + 64],
                                      gx[:, s0, :, :].rearrange("p a r -> p (a r)"), h4[:, :, :, w], start=True, stop=True)
                if w % 8 == 7:
                    mm.then_inc(S["bias_ready"], 1)
            pe.wait_ge(S["v_copied"], 4)
            for r in range(HH):
                s0 = (-r) % KR
                mm = nc.tensor.matmul(ps[0:C, r // 8, (r % 8) * 64:(r % 8) * 64 + 64],
                                      gy[:, s0, :, :].rearrange("p a r -> p (a r)"), h4[:, :, r, :], start=True, stop=True)
                if r % 8 == 7:
                    mm.then_inc(S["bias_ready"], 1)

            def scores(b2, hb, xb, p, early=False):
                pe.wait_ge(S["q_staged"], p + 1)
                if not early:
                    pe.wait_ge(S["exp_done"], p - 1)
                for h in range(2):
                    mm = nc.tensor.matmul(
                        ps[:, 2 * xb + h, 0:NKEY], q_st[:, xb, h, :],
                        k_aug[:, bass.ds(2 * h + b2, 1), bass.ds(BR * hb, KR), BC * xb:BC * xb + KC],
                        start=True, stop=True)
                mm.then_inc(S["scores_ready"], 1)

            def turn_values(pp, p, first=False):
                pe.wait_ge(S["v_staged"], p + 1)
                if not first:
                    pe.wait_ge(S["vk_copied"], p)
                for c in range(NCH):
                    mm = nc.tensor.transpose(ps[0:CH, 6, c * P:c * P + P],
                                             v_st[:, pp, c * CH:c * CH + CH], eye[:])
                mm.then_inc(S["v_turned"], 1)

            def turn_probs(pp, p, first=False):
                pe.wait_ge(S["probs_ready"], p + 1)
                if not first:
                    pe.wait_ge(S["pt_copied"], p)
                for h in range(2):
                    for c in range(NCH):
                        mm = nc.tensor.transpose(ps[0:CH, 4 + h, c * P:c * P + P],
                                                 prob[:, pp, h, c * CH:c * CH + CH], eye[:])
                mm.then_inc(S["probs_turned"], 1)

            def mix(pp, p, first=False):
                pe.wait_ge(S["pt_copied"], p + 1)
                pe.wait_ge(S["vk_copied"], p + 1)
                if not first:
                    pe.wait_ge(S["mixed"], p)
                for c in range(NCH):
                    for h in range(2):
                        mm = nc.tensor.matmul(ps[C * h:C * h + C, 7, 0:P],
                                              v_key[0:CH, pp, c, C * h:C * h + C],
                                              prob_t[0:CH, pp, h, c, :],
                                              start=(c == 0), stop=(c == NCH - 1))
                mm.then_inc(S["pv_done"], 1)

            pe.wait_ge(S["c_loaded"], 16 * 9)
            scores(0, 0, 0, 0, early=True)
            scores(0, 0, 1, 1, early=True)
            turn_values(0, 0, first=True)
            turn_probs(0, 0, first=True)

            def rest_of_first(b2, hb):
                scores(b2, hb, 0, 2)
                turn_values(1, 1)
                mix(0, 0, first=True)
                turn_probs(1, 1)
                scores(b2, hb, 1, 3)
                turn_values(0, 2)
                mix(1, 1)

            rest_of_first(0, 1)
            with pe.Fori(2, 8) as r:
                b2 = pe.snap(r // 4)
                hb = pe.snap(r % 4)
                for xb in range(2):
                    p = 2 * r + xb - 2
                    turn_probs(xb, p)
                    scores(b2, hb, xb, p + 2)
                    turn_values(1 - xb, p + 1)
                    mix(xb, p)
            turn_probs(0, 14)
            turn_values(1, 15)
            mix(0, 14)
            turn_probs(1, 15)
            mix(1, 15)

            pe.wait_ge(S["mixed"], NPAIR)
            norm(x2f, 1)

            def turn_row(n):
                nc.tensor.transpose(ps[0:1, 7, 0:P], h2[:, 0:1], eye[:]).then_inc(S["row_turned"], 1)

            pe.wait_ge(S["normed"], 8)
            turn_row(0)

            def attention(a, f, wrow):
                pe.wait_ge(S["aw_loaded"], 16 * (a + 1))
                pe.sem_inc(S["passed"], 1)
                for h in range(2):
                    nc.tensor.matmul(ps[C * h:C * h + C, 7, 0:C], wa[:, 0, :], wa[:, 1, :],
                                     start=True, stop=True)
                    mm = nc.tensor.matmul(ps[C * h:C * h + C, 6, 0:C], wa[:, 2, :], wa[:, 3, :],
                                          start=True, stop=True)
                mm.then_inc(S["fold_ready"], 1)
                with pe.Fori(0, 2) as b2:
                    i = pe.snap(2 * a + b2)
                    base = pe.snap(NTILE * i)
                    pe.wait_ge(S["h_staged"], i + 1)
                    pe.wait_ge(S["fold_a"], a + 1)
                    pe.wait_ge(S["fold_d"], a + 1)
                    for c in range(2):
                        mm = nc.tensor.matmul(ps[:, 6 + c, :], qk_bd[:], hs[:, c * 512:c * 512 + 512],
                                              start=True, stop=True)
                    mm.then_inc(S["g_ready"], 1)
                    for c in range(NKC):
                        mm = nc.tensor.matmul(ps[:, 4 + c // 4, (c % 4) * P:(c % 4) * P + P],
                                              hs[:, c * P:c * P + P], vo_bd[:], start=True, stop=True)
                    mm.then_inc(S["vo_ready"], 1)

                    def tile_scores(n):
                        if n == 0:
                            pe.wait_ge(S["g_act"], i + 1)
                            pe.wait_ge(S["g_dve"], i + 1)
                        if n >= 2:
                            pe.wait_ge(S["s_exp"], base + n - 1)
                        for c in range(2):
                            mm = nc.tensor.matmul(ps[:, 2 * (n % 2) + c, :],
                                                  g_half[:, n % 2, (n // 2) * P:(n // 2) * P + P],
                                                  hs[:, c * 512:c * 512 + 512], start=True, stop=True)
                        mm.then_inc(S["s_ready"], 1)

                    def tile_turn(n):
                        pe.wait_ge(S["s_prob"], base + n + 1)
                        if n == 0:
                            pe.wait_ge(S["vo_act"], i + 1)
                            pe.wait_ge(S["vo_dve"], i + 1)
                        else:
                            pe.wait_ge(S["s_pta"], base + n)
                            pe.wait_ge(S["s_ptd"], base + n)
                        for c in range(NKC):
                            mm = nc.tensor.transpose(ps[:, 4 + c // 4, (c % 4) * P:(c % 4) * P + P],
                                                     pr[:, n % 2, c * P:c * P + P], eye[:])
                        mm.then_inc(S["s_turned"], 1)

                    tile_scores(0)
                    tile_scores(1)
                    for n in range(NTILE):
                        tile_turn(n)
                        if n + 2 < NTILE:
                            tile_scores(n + 2)
                        if n % 8 == 7:
                            g = n // 8
                            pe.wait_ge(S["s_pta"], base + n + 1)
                            pe.wait_ge(S["s_ptd"], base + n + 1)
                            for c in range(NKC):
                                for h in range(2):
                                    mm = nc.tensor.matmul(ps[C * h:C * h + C, 6 + g, :],
                                                          vk[:, c, C * h:C * h + C],
                                                          prt[:, g, h, c, :],
                                                          start=(c == 0), stop=(c == NKC - 1))
                            mm.then_inc(S["s_pv"], 1)

            def feed_forward(a, f, wrow):
                pe.wait_ge(S["fw_loaded"], 48 * (f + 1))
                pe.wait_ge(S["section_done"], a + f + 1)

                def up(t):
                    for h in range(2):
                        if t > 0:
                            pe.wait_ge(S["relu_act"], 8 * f + 2 * t - 1 + h)
                            pe.wait_ge(S["relu_dve"], 8 * f + 2 * t - 1 + h)
                        for c in range(2):
                            mm = nc.tensor.matmul(ps[:, 2 * h + c, :], w1z[:, h, c * P:c * P + P],
                                                  h2[:, t * 512:t * 512 + 512], start=True, stop=True)
                        mm.then_inc(S["hid_ready"], 1)

                def down(t):
                    pe.wait_ge(S["relu_act"], 8 * f + 2 * t + 2)
                    pe.wait_ge(S["relu_dve"], 8 * f + 2 * t + 2)
                    src = hid if t % 2 == 0 else hid2
                    for c in range(2):
                        for h in range(2):
                            mm = nc.tensor.matmul(ps[C * h:C * h + C, 4 + t, :],
                                                  w2p[:, c * C:c * C + C], src[:, 2 * h + c, :],
                                                  start=(c == 0), stop=(c == 1))
                    mm.then_inc(S["hid_down"], 1)

                up(0)
                for t in range(4):
                    if t < 3:
                        up(t + 1)
                    down(t)

            def decide(a, f, n):
                pe.wait_ge(S["section_done"], a + f + 1)
                turn_row(n)

            routed(pe, attention, feed_forward, decide)

        @block.scalar
        def _(act):
            def norm(k, eps):
                for j in range(4):
                    act.wait_ge(S["centered"], 4 * k + j + 1)
                    nc.scalar.activation(sq[:, j * 512:j * 512 + 512], xc[:, j * 512:j * 512 + 512],
                                         ACT.Square).then_inc(S["squared"], 1)
                for j in range(4):
                    act.wait_ge(S["var_ready"], 4 * k + j + 1)
                    nc.scalar.activation(sq[:, j * 512:j * 512 + 512], ps[:, 4 + j, :], ACT.Sqrt,
                                         bias=eps_c[:, k:k + 1]).then_inc(S["std_ready"], 1)

            act.wait_ge(S["eps_set"], 1)
            act.wait_ge(S["zeroed"], 1)
            norm(0, LN_C_EPS)
            for h in range(2):
                act.wait_ge(S["tab_ready"], 1)
                for tab, at, n in ((gx, 0, KC), (gy, TX, KR)):
                    src = ps[C * h:C * h + C, 0, at:at + 1]
                    shifted = bass.AP(tensor=src.tensor, offset=src.offset,
                                      ap=[list(src.ap[0]), [1, n], [1, 32]])
                    nc.scalar.copy(tab[C * h:C * h + C, :, h, :], shifted
                                   ).then_inc(S["tab_copied"], 1)
            for j in range(4):
                for h in range(2):
                    act.wait_ge(S["qk_ready"], 2 * j + h + 1)
                    nc.scalar.copy(q_aug[0:C, 2 * h + j // 2, 16 * (j % 2):16 * (j % 2) + 16, :],
                                   ps[0:C, 2 * j + h, :].rearrange("p (r w) -> p r w", w=WW)
                                   ).then_inc(S["q_copied"], 1)
            for j in range(4):
                act.wait_ge(S["v_ready"], j + 1)
                r0 = PAD + 16 * (j % 2)
                nc.scalar.copy(v_pad[:, j // 2, r0:r0 + 16, PAD:PAD + WW],
                               ps[:, j, :].rearrange("p (r w) -> p r w", w=WW)
                               ).then_inc(S["v_copied"], 1)

            def exps(pp, p, early=False):
                act.wait_ge(S["negmax_ready"], p + 1)
                if not early:
                    act.wait_ge(S["probs_turned"], p - 1)
                for h in range(2):
                    ins = nc.scalar.activation(prob[:, pp, h, 0:NKEY], ps[:, 2 * pp + h, 0:NKEY],
                                               ACT.Exp, bias=negmax[:, pp, h:h + 1],
                                               accum_out=rowsum[:, pp, h:h + 1])
                ins.then_inc(S["exp_done"], 1)

            def copy_turned(pp, p, early=False):
                act.wait_ge(S["probs_turned"], p + 1)
                if not early:
                    act.wait_ge(S["pv_done"], p - 1)
                for h in range(2):
                    ins = nc.scalar.copy(prob_t[0:CH, pp, h, :, :],
                                         ps[0:CH, 4 + h, 0:NCH * P].rearrange("p (c q) -> p c q", c=NCH))
                ins.then_inc(S["pt_copied"], 1)

            exps(0, 0, early=True)
            exps(1, 1, early=True)
            for pp in range(2):
                copy_turned(pp, pp, early=True)
                exps(pp, pp + 2)
            with act.Fori(1, 7) as r:
                for pp in range(2):
                    copy_turned(pp, 2 * r + pp)
                    exps(pp, 2 * r + pp + 2)
            for pp in range(2):
                copy_turned(pp, 14 + pp)

            norm(1, LN_T_EPS)

            def attention(a, f, wrow):
                act.wait_ge(S["fold_ready"], a + 1)
                for h in range(2):
                    ins = nc.scalar.mul(qk_bd[C * h:C * h + C, C * h:C * h + C],
                                        ps[C * h:C * h + C, 7, 0:C], SCALE)
                ins.then_inc(S["fold_a"], 1)
                with act.Fori(0, 2) as b2:
                    i = act.snap(2 * a + b2)
                    base = act.snap(NTILE * i)
                    act.wait_ge(S["g_ready"], i + 1)
                    nc.scalar.copy(g_half[0:C, 0, :], ps[0:C, 6:8, :]).then_inc(S["g_act"], 1)
                    act.wait_ge(S["vo_ready"], i + 1)
                    nc.scalar.copy(vk[:, 0:4, :], ps[:, 4, :].rearrange("p (c d) -> p c d", c=4)
                                   ).then_inc(S["vo_act"], 1)

                    def exps(n):
                        act.wait_ge(S["s_negmax"], base + n + 1)
                        if n >= 2:
                            act.wait_ge(S["s_turned"], base + n - 1)
                        nc.scalar.activation(pr[:, n % 2, :], ps[:, 2 * (n % 2):2 * (n % 2) + 2, :],
                                             ACT.Exp, bias=negmax[:, 0, n % 2:n % 2 + 1],
                                             accum_out=rowsum[:, 0, n % 2:n % 2 + 1]
                                             ).then_inc(S["s_exp"], 1)

                    exps(0)
                    exps(1)
                    for n in range(NTILE):
                        act.wait_ge(S["s_turned"], base + n + 1)
                        q0 = (n // 2 % 4) * P
                        nc.scalar.copy(prt[:, n // 8, n % 2, 0:4, q0:q0 + P],
                                       ps[:, 4, :].rearrange("p (c q) -> p c q", c=4)
                                       ).then_inc(S["s_pta"], 1)
                        if n + 2 < NTILE:
                            exps(n + 2)

            def feed_forward(a, f, wrow):
                for t in range(4):
                    dst = hid if t % 2 == 0 else hid2
                    for h in range(2):
                        act.wait_ge(S["hid_ready"], 8 * f + 2 * t + h + 1)
                        nc.scalar.activation(dst[:, 2 * h, :], ps[:, 2 * h, :], ACT.Relu,
                                             bias=w2p[:, 2 * C:2 * C + 1]).then_inc(S["relu_act"], 1)

            routed(act, attention, feed_forward)

        @block.vector
        def _(dve):
            nc.vector.memset(eps_c[:, 0:1], LN_C_EPS)
            nc.vector.memset(eps_c[:, 1:2], LN_T_EPS).then_inc(S["eps_set"], 1)
            dve.wait_ge(S["x_loaded"], 48)

            def norm(src, k):
                for j in range(4):
                    s = slice(j * 512, j * 512 + 512)
                    dve.wait_ge(S["mean_ready"], 4 * k + j + 1)
                    nc.vector.tensor_tensor(xc[:, s], src[:, s], ps[:, j, :], ALU.subtract
                                            ).then_inc(S["centered"], 1)
                for j in range(4):
                    s = slice(j * 512, j * 512 + 512)
                    dve.wait_ge(S["std_ready"], 4 * k + j + 1)
                    nc.vector.reciprocal(sq[:, s], sq[:, s]).then_inc(S["rstd_ready"], 1)
                    dve.wait_ge(S["rstd_ready"], 4 * k + j + 1)
                    dve.wait_ge(S["centered"], 4 * k + j + 1)
                    nc.vector.tensor_tensor(h2[:, s], xc[:, s], sq[:, s], ALU.mult
                                            ).then_inc(S["normed"], 1)

            norm(x2f, 0)
            for j in range(4):
                for h in range(2):
                    dve.wait_ge(S["qk_ready"], 2 * j + h + 1)
                    r0 = PAD + 16 * (j % 2)
                    nc.vector.tensor_copy(k_aug[0:C, 2 * h + j // 2, r0:r0 + 16, PAD:PAD + WW],
                                          ps[C:P, 2 * j + h, :].rearrange("p (r w) -> p r w", w=WW)
                                          ).then_inc(S["k_copied"], 1)
            dve.wait_ge(S["c_loaded"], 16 * 9)
            for k in range(8):
                dve.wait_ge(S["bias_ready"], k + 1)
                for h in range(2):
                    rows = slice(32 * h, 32 * h + 32)
                    if k < 4:
                        bank, src0, dst0 = 4 + k, 8 * k, XROW
                        dst = q_aug[dst0:dst0 + 32, 2 * h:2 * h + 2, :, 8 * k:8 * k + 8].rearrange(
                            "p a r w -> p w a r")
                        got = ps[rows, bank, :].rearrange("p (w a r) -> p w a r", w=8, a=2)
                        mask = mask_x[rows, 8 * k:8 * k + 8]
                        shape = [32, 8, 2, HH]
                    else:
                        bank, r0, dst0 = k - 4, 8 * (k - 4), YROW
                        dst = q_aug[dst0:dst0 + 32, 2 * h:2 * h + 2, r0:r0 + 8, :].rearrange(
                            "p a r w -> p r a w")
                        got = ps[rows, bank, :].rearrange("p (r a w) -> p r a w", r=8, a=2)
                        mask = mask_x[rows, WW + r0:WW + r0 + 8]
                        shape = [32, 8, 2, WW]
                    nc.vector.tensor_tensor(dst, got, mask.unsqueeze(2).unsqueeze(3).broadcast_to(shape),
                                            ALU.add).then_inc(S["bias_added"], 1)

            def maxima(pp, p):
                dve.wait_ge(S["scores_ready"], p + 1)
                nc.vector.tensor_reduce(negmax[:, pp, :], ps[:, 2 * pp:2 * pp + 2, 0:NKEY], X, ALU.max,
                                        negate=True).then_inc(S["negmax_ready"], 1)

            def normalise(pp, p):
                dve.wait_ge(S["exp_done"], p + 1)
                nc.vector.reciprocal(rinv[:, pp, :], rowsum[:, pp, :]).then_inc(S["rinv_ready"], 1)
                dve.wait_ge(S["rinv_ready"], p + 1)
                for h in range(2):
                    ins = nc.vector.tensor_scalar(prob[:, pp, h, 0:NKEY], prob[:, pp, h, 0:NKEY],
                                                  rinv[:, pp, h:h + 1], None, ALU.mult)
                ins.then_inc(S["probs_ready"], 1)

            def copy_values(pp, p, early=False):
                dve.wait_ge(S["v_turned"], p + 1)
                if not early:
                    dve.wait_ge(S["pv_done"], p - 1)
                nc.vector.tensor_copy(v_key[0:CH, pp, :, :],
                                      ps[0:CH, 6, 0:NCH * P].rearrange("p (c d) -> p c d", c=NCH)
                                      ).then_inc(S["vk_copied"], 1)

            def add_mixed(b2, hb, xb, p):
                dve.wait_ge(S["pv_done"], p + 1)
                win = x2[:, bass.ds(b2, 1), bass.ds(BR * hb, BR), BC * xb:BC * xb + BC]
                nc.vector.tensor_tensor(win, win,
                                        ps[:, 7, 0:P].rearrange("p (a r c) -> p a r c", a=1, c=BC),
                                        ALU.add).then_inc(S["mixed"], 1)

            maxima(0, 0)
            maxima(1, 1)
            normalise(0, 0)
            copy_values(0, 0, early=True)
            normalise(1, 1)
            maxima(0, 2)
            copy_values(1, 1, early=True)
            add_mixed(0, 0, 0, 0)
            normalise(0, 2)
            maxima(1, 3)
            copy_values(0, 2)
            add_mixed(0, 0, 1, 1)
            with dve.Fori(1, 7) as r:
                b2 = dve.snap(r // 4)
                hb = dve.snap(r % 4)
                for xb in range(2):
                    p = 2 * r + xb
                    normalise(1 - xb, p + 1)
                    maxima(xb, p + 2)
                    copy_values(1 - xb, p + 1)
                    add_mixed(b2, hb, xb, p)
            normalise(1, 15)
            copy_values(1, 15)
            add_mixed(1, 3, 0, 14)
            add_mixed(1, 3, 1, 15)
            dve.wait_ge(S["mixed"], NPAIR)

            norm(x2f, 1)

            steps = [0]

            def step(ins):
                steps[0] += 1
                ins.then_inc(S["dve_step"], 1)
                dve.wait_ge(S["dve_step"], steps[0])

            io_op, io_b, io_m = iota[:, 0:NOPS], iota[:, NOPS:NOPS + NB], iota[:, NOPS + NB:]
            kf = kinds.rearrange("o b k -> o (b k)")
            step(nc.vector.tensor_copy(kf[:], masks8[:, 0, :]))
            step(nc.vector.tensor_copy(fm_f[:], masks8[:, 1, :]))
            step(nc.vector.scalar_tensor_tensor(kf[:], fm_f[:], 2.0, kf[:], ALU.mult, ALU.add))
            step(nc.vector.memset(sc[:, 1:2], 0.0))
            N_DECIDE = 19

            def decide(n, first):
                dve.wait_ge(S["row_turned"], n + 1)
                count = [0]

                def then(ins):
                    count[0] += 1
                    ins.then_inc(S["dve_step"], 1)
                    dve.wait_ge(S["dve_step"], steps[0] + N_DECIDE * n + count[0])

                then(nc.vector.tensor_copy(row[:, 0:NOPS], ps[0:1, 7, 0:NOPS]))
                dve.sem_inc(S["passed"], 1)
                then(nc.vector.max(top8[:], row[:, 0:NOPS]))
                dve.sem_inc(S["passed"], 1)
                then(nc.vector.max_index(idx8[:], top8[:], row[:, 0:NOPS]))
                then(nc.vector.tensor_copy(sc[:, 0:1], idx8[:, 0:1]))
                then(nc.vector.tensor_scalar(onehot[:], io_op, sc[:, 0:1], None, ALU.is_equal))
                then(nc.vector.tensor_tensor(picked[:], kinds[:],
                                             onehot[:].unsqueeze(1).broadcast_to([1, NB, NOPS]), ALU.mult))
                then(nc.vector.tensor_reduce(rw[:, 0, :], picked[:], X, ALU.add))
                then(nc.vector.tensor_scalar(rw[:, 1, :], rw[:, 0, :], 0.0, None, ALU.is_gt))
                then(nc.vector.scalar_tensor_tensor(rw[:, 2, :], io_b, sc[:, 1:2], rw[:, 1, :],
                                                    ALU.is_ge, ALU.mult))
                then(nc.vector.tensor_tensor(rw[:, 1, :], rw[:, 2, :], io_m, ALU.mult))
                then(nc.vector.tensor_reduce(sc[:, 2:3], rw[:, 1, :], X, ALU.min))
                then(nc.vector.tensor_scalar(sc[:, 4:5], sc[:, 2:3], float(NB), None, ALU.add))
                then(nc.vector.tensor_scalar(sc[:, 1:2], sc[:, 4:5], 1.0, None, ALU.add))
                then(nc.vector.scalar_tensor_tensor(rw[:, 3, :], io_b, sc[:, 4:5], rw[:, 0, :],
                                                    ALU.is_equal, ALU.mult))
                then(nc.vector.tensor_reduce(sc[:, 3:4], rw[:, 3, :], X, ALU.add))
                then(nc.vector.tensor_scalar(sc[:, 7:8], sc[:, 3:4], 1.5, None, ALU.is_gt))
                then(nc.vector.scalar_tensor_tensor(sc[:, 6:7], sc[:, 7:8], -2.0, sc[:, 3:4],
                                                    ALU.mult, ALU.add))
                then(nc.vector.scalar_tensor_tensor(sc[:, 5:6], sc[:, 4:5], float(NOPS), sc[:, 0:1],
                                                    ALU.mult, ALU.add))
                if not first:
                    dve.wait_ge(S["info_read"], 5 * n)
                then(nc.vector.tensor_copy(info[:], sc[:, 4:8]))
                assert count[0] == N_DECIDE
                dve.sem_inc(S["decided"], 1)

            dve.sem_inc(S["section_done"], 1)
            decide(0, True)

            def attention(a, f, wrow):
                dve.wait_ge(S["fold_ready"], a + 1)
                for h in range(2):
                    ins = nc.vector.tensor_copy(vo_bd[C * h:C * h + C, C * h:C * h + C],
                                                ps[C * h:C * h + C, 6, 0:C])
                ins.then_inc(S["fold_d"], 1)
                with dve.Fori(0, 2) as b2:
                    i = dve.snap(2 * a + b2)
                    base = dve.snap(NTILE * i)
                    nc.vector.tensor_scalar(hs, h2[:, bass.ds(b2 * NPOS, NPOS)], ones_c[:], None, ALU.mult).then_inc(S["h_staged"], 1)
                    dve.wait_ge(S["g_ready"], i + 1)
                    nc.vector.tensor_copy(g_half[C:P, 1, :], ps[C:P, 6:8, :]).then_inc(S["g_dve"], 1)
                    dve.wait_ge(S["vo_ready"], i + 1)
                    nc.vector.tensor_copy(vk[:, 4:8, :], ps[:, 5, :].rearrange("p (c d) -> p c d", c=4)
                                          ).then_inc(S["vo_dve"], 1)

                    def maxima(n):
                        dve.wait_ge(S["s_ready"], base + n + 1)
                        nc.vector.tensor_reduce(negmax[:, 0, n % 2:n % 2 + 1],
                                                ps[:, 2 * (n % 2):2 * (n % 2) + 2, :],
                                                mybir.AxisListType.XY, ALU.max, negate=True
                                                ).then_inc(S["s_negmax"], 1)

                    def normalise(n):
                        dve.wait_ge(S["s_exp"], base + n + 1)
                        nc.vector.reciprocal(rinv[:, 0, n % 2:n % 2 + 1], rowsum[:, 0, n % 2:n % 2 + 1]
                                             ).then_inc(S["s_rinv"], 1)
                        dve.wait_ge(S["s_rinv"], base + n + 1)
                        nc.vector.tensor_scalar(pr[:, n % 2, :], pr[:, n % 2, :],
                                                rinv[:, 0, n % 2:n % 2 + 1], None, ALU.mult
                                                ).then_inc(S["s_prob"], 1)

                    def store(g):
                        dve.wait_ge(S["s_pv"], 2 * i + g + 1)
                        nc.vector.tensor_scalar(h2[:, bass.ds(b2 * NPOS + g * 512, 512)], ps[:, 6 + g, :],
                                                ones_c[:], None, ALU.mult).then_inc(S["z_ready"], 1)

                    maxima(0)
                    maxima(1)
                    normalise(0)
                    for n in range(NTILE):
                        if n + 1 < NTILE:
                            normalise(n + 1)
                        dve.wait_ge(S["s_turned"], base + n + 1)
                        q0 = (n // 2 % 4) * P
                        nc.vector.tensor_copy(prt[:, n // 8, n % 2, 4:8, q0:q0 + P],
                                              ps[:, 5, :].rearrange("p (c q) -> p c q", c=4)
                                              ).then_inc(S["s_ptd"], 1)
                        if n + 2 < NTILE:
                            maxima(n + 2)
                        if n == 10:
                            store(0)
                    store(1)
                dve.wait_ge(S["z_ready"], 4 * a + 4 + 4 * f)
                dve.sem_inc(S["section_done"], 1)

            def feed_forward(a, f, wrow):
                def relu(t, h):
                    dst = hid if t % 2 == 0 else hid2
                    dve.wait_ge(S["hid_ready"], 8 * f + 2 * t + h + 1)
                    nc.vector.tensor_scalar(dst[:, 2 * h + 1, :], ps[:, 2 * h + 1, :],
                                            w2p[:, 2 * C + 1:2 * C + 2], 0.0, ALU.add, ALU.max
                                            ).then_inc(S["relu_dve"], 1)

                def store(t):
                    dve.wait_ge(S["hid_down"], 4 * f + t + 1)
                    nc.vector.tensor_scalar(h2[:, t * 512:t * 512 + 512], ps[:, 4 + t, :],
                                            w2p[:, 2 * C + 2:2 * C + 3], None, ALU.add
                                            ).then_inc(S["z_ready"], 1)

                relu(0, 0)
                relu(0, 1)
                for t in range(4):
                    if t < 3:
                        relu(t + 1, 0)
                        relu(t + 1, 1)
                    store(t)
                dve.wait_ge(S["z_ready"], 4 * a + 4 * f + 4)
                dve.sem_inc(S["section_done"], 1)

            routed(dve, attention, feed_forward, lambda a, f, n: decide(n, False))
            for j in range(4):
                s = slice(j * 512, j * 512 + 512)
                nc.vector.tensor_tensor(xc[:, s], x2f[:, s], h2[:, s], ALU.add
                                        ).then_inc(S["out_ready"], 1)


def constants():
    import numpy as np

    key_onehot = np.zeros((C, HP, WP), np.float32)
    for r in range(KC):
        key_onehot[r, :, r::KC] = 1.0
    for r in range(KR):
        key_onehot[YROW - XROW + r, r::KR, :] = 1.0
    masks = np.zeros((P, WW + HH), np.float32)
    for h in range(2):
        for r in range(KC):
            for w in range(WW):
                masks[32 * h + r, w] = 0.0 if (r - w) % KC < KS else -1e30
        for r in range(KR):
            for y in range(HH):
                masks[32 * h + r, WW + y] = 0.0 if (r - y) % KR < KS else -1e30
    ident = np.eye(P, dtype=np.float32)
    mean_mat = np.kron(np.eye(2), np.full((C, C), 1.0 / C)).astype(np.float32)
    iotas = np.concatenate([np.arange(NOPS), np.arange(NB), np.arange(NB) - NB])[None].astype(np.float32)
    return key_onehot, masks, ident, mean_mat, iotas


def kernel(x, L0_conv_wq, L0_conv_wk, L0_conv_wv, L0_conv_rel_x, L0_conv_rel_y,
           L0_ffn_ffn_w1, L0_ffn_ffn_b1, L0_ffn_ffn_w2, L0_ffn_ffn_b2,
           L0_ffn_wq, L0_ffn_wk, L0_ffn_wv, L0_ffn_wo, L0_ffn_attn_mask, L0_ffn_ffn_mask):
    import numpy as np
    import concourse.bacc as bacc
    from concourse.bass_utils import run_bass_kernel_spmd

    x = np.ascontiguousarray(x)
    wq, wk, wv = (np.asarray(w) for w in (L0_conv_wq, L0_conv_wk, L0_conv_wv))
    rel_x, rel_y = np.asarray(L0_conv_rel_x), np.asarray(L0_conv_rel_y)
    tables = np.zeros((C, TX + TY), np.float32)
    half = rel_x.shape[0]
    for c in range(C):
        d = c % (2 * half)
        table, rel, period, length, at = ((0, rel_x, KC, TX, 0) if d < half else (1, rel_y, KR, TY, TX))
        for t in range(length):
            if t % period < KS:
                tables[c, at + t] = rel[d % half, t % period]
    n = NB * NOPS
    flat = lambda w: np.asarray(w).reshape((n,) + np.asarray(w).shape[2:])
    turned = lambda w: flat(w).transpose(0, 2, 1)
    attn_pack = np.ascontiguousarray(np.stack(
        [turned(L0_ffn_wq), turned(L0_ffn_wk), turned(L0_ffn_wv), flat(L0_ffn_wo)], axis=2))
    w2 = flat(L0_ffn_ffn_w2).reshape(n, 2, P, C).transpose(0, 2, 1, 3).reshape(n, P, 2 * C)
    b1 = flat(L0_ffn_ffn_b1).reshape(n, 2, P).transpose(0, 2, 1)
    b2 = np.concatenate([flat(L0_ffn_ffn_b2)] * 2, axis=1)[:, :, None]
    ffn_pack = np.ascontiguousarray(np.concatenate([w2, b1, b2], axis=2))
    key_onehot, masks, ident, mean_mat, iotas = constants()
    arrays = {
        "x": x,
        "w_qk": np.ascontiguousarray(np.concatenate([wq.T, wk.T], axis=1)),
        "w_q": np.ascontiguousarray(wq),
        "w_v": np.ascontiguousarray(wv.T),
        "bias_tables": tables,
        "key_onehot": key_onehot, "masks": masks, "ident": ident, "mean_mat": mean_mat, "iotas": iotas,
        "attn_mask": np.ascontiguousarray(np.asarray(L0_ffn_attn_mask)).reshape(1, n),
        "ffn_mask": np.ascontiguousarray(np.asarray(L0_ffn_ffn_mask)).reshape(1, n),
        "attn_pack": attn_pack,
        "ffn_w1": np.ascontiguousarray(flat(L0_ffn_ffn_w1)),
        "ffn_pack": ffn_pack,
    }
    nc = bacc.Bacc("TRN2", target_bir_lowering=False, num_devices=1)
    handles = {k: nc.dram_tensor(f"in_{k}", a.shape, mybir.dt.from_np(a.dtype), kind="ExternalInput").ap()
               for k, a in arrays.items()}
    out = nc.dram_tensor("out", x.shape, F32, kind="ExternalOutput").ap()
    build(nc, out=out, **handles)
    r = run_bass_kernel_spmd(nc, [{f"in_{k}": a for k, a in arrays.items()}], core_ids=[0])
    return r.results[0]["out"]
```

```python
from contextlib import ExitStack

import concourse.bass as bass
from concourse import mybir

F32 = mybir.dt.float32
F32R = mybir.dt.float32r
I32 = mybir.dt.int32
U32 = mybir.dt.uint32
U8 = mybir.dt.uint8
ALU = mybir.AluOpType
ACT = mybir.ActivationFunctionType
X = mybir.AxisListType.X

P = 128
C = 64
HH, WW = 32, 32
NPOS = HH * WW
COLS = 2 * NPOS
KS, PAD = 7, 3
HP, WP = HH + 2 * PAD, WW + 2 * PAD
BR, BC = 8, 16
KR, KC = BR + KS - 1, BC + KS - 1
NKEY = KR * KC
NCH, CH = 3, 103
NPAIR = 16
XROW, YROW = 64, 96
TX, TY = 32 + KC - 1, 32 + KR - 1
NB, NOPS, HID = 33, 19, 256
NTILE = 16
NT = 2 * NTILE
NKC = NPOS // P
SCALE = float(C) ** -0.5
LN_C_EPS, LN_T_EPS = 1e-6, 1e-5
VBANK, QKBANK = (4, 5, 6, 0), (1, 2, 3, 7, 4, 5, 6, 0)
ROUNDS = (4, 3, 3)
W2COLS = 2 * C + 2 + 1


def build(nc, x, w_qk, w_q, w_v, bias_tables, key_onehot, masks, ident, mean_mat, spread_mat, iotas,
          attn_mask, ffn_mask, attn_pack, ffn_w1, ffn_pack, out):
    with ExitStack() as ctx:
        def sb(name, shape, dt=F32):
            return ctx.enter_context(nc.sbuf_tensor(name, shape, dt))

        def sem(name):
            return ctx.enter_context(nc.semaphore(name))

        ps = ctx.enter_context(nc.psum_tensor("ps", [P, 8, 512], F32))

        eye = sb("eye", [P, P])
        mean_w = sb("mean_w", [P, P + 2 * 32])
        spread_w = sb("spread_w", [P, 8, P])
        mask_x = sb("mask_x", [P, WW + HH])
        wqk = sb("wqk", [P, 2, P])
        wq_nat = sb("wq_nat", [C, C])
        wv_bd = sb("wv_bd", [P, P])
        rel_tab = sb("rel_tab", [C, TX + TY])
        gx = sb("gx", [P, KC, 2, 32])
        gy = sb("gy", [P, KR, 2, 32])
        eps_c = sb("eps_c", [P, 2])
        ones_c = sb("ones_c", [P, 1])
        spare = sb("spare", [P, 1])
        x2 = sb("x2", [P, 2, HH, WW])
        xc = sb("xc", [P, COLS])
        sq = sb("sq", [P, COLS])
        h2 = sb("h2", [P, COLS])
        arena = sb("arena", [P, 2 * 2 * NKC * 512])
        n_q, n_k, n_v = 4 * NPOS, 4 * HP * WP, 2 * HP * WP
        q_aug = arena[:, 0:n_q].rearrange("p (a h w) -> p a h w", a=4, w=WW)
        k_aug = arena[:, n_q:n_q + n_k].rearrange("p (a h w) -> p a h w", a=4, w=WP)
        v_pad = arena[:, n_q + n_k:n_q + n_k + n_v].rearrange("p (a h w) -> p a h w", a=2, w=WP)
        prt = arena.rearrange("p (a b c q) -> p a b c q", a=2, b=2, c=NKC)
        q_st = sb("q_st", [P, 2, 2, BR * BC])
        v_st = sb("v_st", [P, 2, NCH * CH])
        v_key = sb("v_key", [P, 2, NCH, P])
        prob = sb("prob", [P, 2, 2, NCH * CH])
        prob_t = sb("prob_t", [P, 2, 2, NCH, P])
        negmax = sb("negmax", [P, 2, 2])
        rowsum = sb("rowsum", [P, 2, 2])
        rinv = sb("rinv", [P, 2, 2])
        masks8 = sb("masks8", [NOPS, 2, NB], U8)
        kinds = sb("kinds", [NOPS, 2, NB])
        iota = sb("iota", [NOPS, NB])
        ahead = sb("ahead", [NOPS, 2, 2 * NB])
        ahead_i = sb("ahead_i", [NOPS, NB + 1], I32)
        table = sb("table", [1, NOPS * (NB + 1)], I32)
        top8 = sb("top8", [1, 8])
        idx8 = sb("idx8", [1, 8], U32)
        wa = sb("wa", [C, 4, C])
        qk_bd = sb("qk_bd", [P, P])
        vo_bd = sb("vo_bd", [P, P])
        h_st = sb("h_st", [P, 2, 2, 2, NPOS], F32R)
        g_st = sb("g_st", [P, 2, 2, NPOS], F32R)
        h_f, g_f = h_st.bitcast(F32), g_st.bitcast(F32)
        vk = sb("vk", [P, 2, NKC, P])
        pr = sb("pr", [P, 2, NPOS])
        w1d = sb("w1d", [P, HID])
        w1_hi = sb("w1_hi", [P, HID], F32R)
        w1_st = sb("w1_st", [P, HID], F32R)
        w2p = sb("w2p", [P, W2COLS])
        hid = xc.rearrange("p (a b) -> p a b", a=4)
        hid2 = sq.rearrange("p (a b) -> p a b", a=4)

        next_steps = nc.dram_tensor("next_steps", (NOPS, NB + 1), I32, kind="Internal").ap()

        names = """x_loaded w_loaded c_loaded m_loaded s_loaded zeroed w_zeroed eps_set
            mean_ready centered squared var_ready std_ready rstd_ready normed
            tab_ready tab_copied qk_ready q_copied k_copied v_ready v_copied bias_ready bias_added
            q_staged v_staged scores_ready negmax_ready exp_done rinv_ready probs_ready
            probs_turned pt_copied v_turned vk_copied pv_done mixed spread_ready
            row_turned dve_step op_max decided passed info_read section_done ffn_done
            table_ready table_spilled table_loaded inv_ready
            aw_loaded fw_loaded fold_ready fold_a fold_d
            part_act part_dve g_ready g_high g_low vo_ready vo_copied
            s_ready s_negmax s_exp s_rinv s_prob s_turned s_pt s_pv a_stored
            w1_act w1_dve f_act f_dve hid_ready relu_act relu_dve hid_down z_ready
            out_ready stored_0 stored_1""".split()
        S = {n: sem(n) for n in names}

        x_half = [x[2 * h:2 * h + 2].rearrange("b c r w -> c b r w") for h in range(2)]
        o_half = [out[2 * h:2 * h + 2].rearrange("b c r w -> c b (r w)") for h in range(2)]
        x2f = x2.rearrange("p a h w -> p (a h w)")

        block = ctx.enter_context(nc.Block())

        readers = 4

        def routed(eng, attention, feed_forward):
            name = eng.engine.name
            op, entry, step, cur, am, fm, n_att, n_ffn, event = (
                eng.alloc_register(f"{name}_{k}")
                for k in "op entry step cur am fm n_att n_ffn event".split())
            for reg in (n_att, n_ffn, event, cur):
                eng.reg_mov(reg, 0)

            def load_next():
                done = eng.snap(n_att, min_val=0, max_val=NB) + eng.snap(n_ffn, min_val=0, max_val=NB)
                eng.wait_ge(S["decided"], done + 1)
                eng.sem_inc(S["passed"], 1)
                eng.load(op, idx8[0:1, 0:1])
                at = (eng.snap(op, min_val=0, max_val=NOPS - 1) * (NB + 1)
                      + eng.snap(cur, min_val=0, max_val=NB))
                eng.load(entry, table[0:1, bass.ds(at, 1)])
                eng.sem_inc(S["info_read"], 1)
                eng.reg_alu(step, entry, 2, op=ALU.arith_shift_right)
                eng.reg_alu(am, entry, 1, op=ALU.bitwise_and)
                eng.reg_alu(fm, entry, 2, op=ALU.bitwise_and)
                eng.reg_add(cur, step, 1)

            def run_event():
                row = eng.snap(eng.snap(step, min_val=0, max_val=NB - 1) * NOPS
                               + eng.snap(op, min_val=0, max_val=NOPS - 1))
                ev = eng.snap(event, min_val=0, max_val=NB)
                with eng.If(eng.snap(am, min_val=0, max_val=1) > 0):
                    a = eng.snap(n_att, min_val=0, max_val=NB - 1)
                    f = eng.snap(n_ffn, min_val=0, max_val=NB - 1)
                    attention(a, f, ev, row)
                    eng.reg_add(n_att, n_att, 1)
                with eng.If(eng.snap(fm, min_val=0, max_val=2) > 0):
                    a = eng.snap(n_att, min_val=0, max_val=NB)
                    f = eng.snap(n_ffn, min_val=0, max_val=NB - 1)
                    feed_forward(a, f, ev, row)
                    eng.reg_add(n_ffn, n_ffn, 1)
                eng.reg_add(event, event, 1)
                load_next()

            def rounds(counts):
                with eng.Fori(0, counts[0]):
                    with eng.If(eng.snap(step, min_val=0, max_val=NB) < NB):
                        if len(counts) > 1:
                            rounds(counts[1:])
                        else:
                            run_event()

            eng.wait_ge(S["table_loaded"], 16)
            load_next()
            rounds(ROUNDS)

        def store_output(eng, h):
            for j in range(4):
                eng.wait_ge(S["out_ready"], j + 1)
                eng.dma_start(o_half[h][:, j // 2, (j % 2) * 512:(j % 2) * 512 + 512],
                              xc[C * h:C * h + C, j * 512:j * 512 + 512]).then_inc(S[f"stored_{h}"], 16)
            eng.wait_ge(S[f"stored_{h}"], 16 * 4)

        @block.sync
        def _(sp):
            sp.dma_start(x2[0:C], x_half[0]).then_inc(S["x_loaded"], 16)
            sp.dma_start(mean_w[:], mean_mat).then_inc(S["x_loaded"], 16)
            sp.wait_ge(S["w_zeroed"], 1)
            for h in range(2):
                sp.dma_start(wv_bd[C * h:C * h + C, C * h:C * h + C], w_v).then_inc(S["w_loaded"], 16)
            for h in range(2):
                sp.dma_start(wqk[C * h:C * h + C, h, :], w_qk).then_inc(S["w_loaded"], 16)
            sp.dma_start(mask_x[:], masks).then_inc(S["c_loaded"], 16)
            for b in range(4):
                sp.dma_start(k_aug[C:P, b, :, :], key_onehot).then_inc(S["c_loaded"], 16)
            sp.wait_ge(S["table_ready"], 1)
            sp.dma_start(next_steps, ahead_i[:]).then_inc(S["table_spilled"], 16)
            sp.wait_ge(S["table_spilled"], 16)
            sp.dma_start(table[:], next_steps.rearrange("p n -> (p n)").unsqueeze(0)
                         ).then_inc(S["table_loaded"], 16)

            def attention(a, f, ev, row):
                sp.wait_ge(S["fold_d"], a + 1)
                sp.dma_start(wa[:], attn_pack[bass.ds(row, 1)].rearrange("o c k d -> (o c) k d")
                             ).then_inc(S["aw_loaded"], 16)

            def feed_forward(a, f, ev, row):
                sp.wait_ge(S["ffn_done"], f + 1)
                for h in range(2):
                    sp.dma_start(w1d[C * h:C * h + C, :],
                                 ffn_w1[bass.ds(row, 1)].rearrange("o c k -> (o c) k")
                                 ).then_inc(S["fw_loaded"], 16)
                sp.dma_start(w2p[:], ffn_pack[bass.ds(row, 1)].rearrange("o p k -> (o p) k")
                             ).then_inc(S["fw_loaded"], 16)

            routed(sp, attention, feed_forward)
            store_output(sp, 0)

        @block.gpsimd
        def _(pool):
            nc.gpsimd.memset(ones_c[:], 1.0)
            nc.gpsimd.memset(wqk[:], 0.0)
            nc.gpsimd.memset(wv_bd[:], 0.0).then_inc(S["w_zeroed"], 1)
            nc.gpsimd.memset(gx[:], 0.0)
            nc.gpsimd.memset(gy[:], 0.0)
            nc.gpsimd.memset(k_aug[0:C], 0.0)
            nc.gpsimd.memset(v_pad[:], 0.0)
            nc.gpsimd.memset(v_st[:], 0.0)
            nc.gpsimd.memset(prob[:], 0.0)
            nc.gpsimd.memset(qk_bd[:], 0.0)
            nc.gpsimd.memset(vo_bd[:], 0.0).then_inc(S["zeroed"], 1)

            def stage(b2, hb, xb, p, early=False):
                if early:
                    if xb == 0:
                        pool.wait_ge(S["q_copied"], 8)
                        pool.wait_ge(S["bias_added"], 16)
                        pool.wait_ge(S["v_copied"], 4)
                else:
                    pool.wait_ge(S["scores_ready"], p - 1)
                for h in range(2):
                    src = q_aug[:, bass.ds(2 * h + b2, 1), bass.ds(BR * hb, BR), BC * xb:BC * xb + BC]
                    ins = nc.gpsimd.tensor_tensor(
                        q_st[:, xb, h, :].rearrange("p (a r c) -> p a r c", a=1, c=BC), src,
                        ones_c[:].unsqueeze(2).unsqueeze(3).broadcast_to([P, 1, BR, BC]), ALU.mult)
                ins.then_inc(S["q_staged"], 1)
                if not early:
                    pool.wait_ge(S["v_turned"], p - 1)
                src = v_pad[:, bass.ds(b2, 1), bass.ds(BR * hb, KR), BC * xb:BC * xb + KC]
                nc.gpsimd.tensor_tensor(
                    v_st[:, xb, 0:NKEY].rearrange("p (a r c) -> p a r c", a=1, c=KC), src,
                    ones_c[:].unsqueeze(2).unsqueeze(3).broadcast_to([P, 1, KR, KC]), ALU.mult
                    ).then_inc(S["v_staged"], 1)

            for xb in range(2):
                stage(0, 0, xb, xb, early=True)
            with pool.Fori(1, 8) as r:
                b2 = pool.snap(r // 4)
                hb = pool.snap(r % 4)
                for xb in range(2):
                    stage(b2, hb, xb, 2 * r + xb)


        @block.tensor
        def _(pe):
            def norm(src, k):
                for j in range(4):
                    nc.tensor.matmul(ps[:, j, :], mean_w[:, 0:P], src[:, j * 512:j * 512 + 512],
                                     start=True, stop=True).then_inc(S["mean_ready"], 1)
                for j in range(4):
                    pe.wait_ge(S["squared"], 4 * k + j + 1)
                    for slot in range(2):
                        s0 = (2 * j + slot) * 256
                        mm = nc.tensor.matmul(ps[32 * j:32 * j + 32, 4, 0:256],
                                              mean_w[:, P + 32 * slot:P + 32 * slot + 32],
                                              sq[:, s0:s0 + 256], start=(slot == 0), stop=(slot == 1))
                mm.then_inc(S["var_ready"], 1)
                if k == 0:
                    pe.wait_ge(S["s_loaded"], 16)
                pe.wait_ge(S["inv_ready"], k + 1)
                for j in range(4):
                    for slot in range(2):
                        mm = nc.tensor.matmul(ps[:, j, 256 * slot:256 * slot + 256],
                                              spread_w[:, 2 * j + slot, :], sq[:, 0:256],
                                              start=True, stop=True)
                    mm.then_inc(S["spread_ready"], 1)

            pe.wait_ge(S["x_loaded"], 48)
            norm(x2f, 0)

            pe.wait_ge(S["w_loaded"], 96)
            for j in range(4):
                pe.wait_ge(S["normed"], j + 1)
                nc.tensor.matmul(ps[:, VBANK[j], :], wv_bd[:], h2[:, j * 512:j * 512 + 512],
                                 start=True, stop=True).then_inc(S["v_ready"], 1)
                if j == 0:
                    for h in range(2):
                        mm = nc.tensor.matmul(ps[C * h:C * h + C, 7, 0:TX + TY], wq_nat[:], rel_tab[:],
                                              start=True, stop=True)
                    mm.then_inc(S["tab_ready"], 1)
            for j in range(4):
                for h in range(2):
                    k = 2 * j + h
                    if k == 3:
                        pe.wait_ge(S["tab_copied"], 4)
                    if k > 3:
                        pe.wait_ge(S["v_copied"], k - 3)
                    nc.tensor.matmul(ps[:, QKBANK[k], :], wqk[:, h, :], h2[:, j * 512:j * 512 + 512],
                                     start=True, stop=True).then_inc(S["qk_ready"], 1)
            h4 = h2.rearrange("p (a h w) -> p a h w", a=2, w=WW)
            for w in range(WW):
                if w % 8 == 0:
                    pe.wait_ge(S["q_copied"], w // 8 + 1)
                    pe.wait_ge(S["k_copied"], w // 8 + 1)
                s0 = (-w) % KC
                mm = nc.tensor.matmul(ps[0:C, QKBANK[w // 8], (w % 8) * 64:(w % 8) * 64 + 64],
                                      gx[:, s0, :, :].rearrange("p a r -> p (a r)"), h4[:, :, :, w], start=True, stop=True)
                if w % 8 == 7:
                    mm.then_inc(S["bias_ready"], 1)
            for r in range(HH):
                if r % 8 == 0:
                    pe.wait_ge(S["q_copied"], r // 8 + 5)
                    pe.wait_ge(S["k_copied"], r // 8 + 5)
                s0 = (-r) % KR
                mm = nc.tensor.matmul(ps[0:C, QKBANK[4 + r // 8], (r % 8) * 64:(r % 8) * 64 + 64],
                                      gy[:, s0, :, :].rearrange("p a r -> p (a r)"), h4[:, :, r, :], start=True, stop=True)
                if r % 8 == 7:
                    mm.then_inc(S["bias_ready"], 1)

            def scores(b2, hb, xb, p, early=False):
                pe.wait_ge(S["q_staged"], p + 1)
                if not early:
                    pe.wait_ge(S["exp_done"], p - 1)
                for h in range(2):
                    mm = nc.tensor.matmul(
                        ps[:, 2 * xb + h, 0:NKEY], q_st[:, xb, h, :],
                        k_aug[:, bass.ds(2 * h + b2, 1), bass.ds(BR * hb, KR), BC * xb:BC * xb + KC],
                        start=True, stop=True)
                mm.then_inc(S["scores_ready"], 1)

            def turn_values(pp, p, first=False):
                pe.wait_ge(S["v_staged"], p + 1)
                if not first:
                    pe.wait_ge(S["vk_copied"], p)
                for c in range(NCH):
                    mm = nc.tensor.transpose(ps[0:CH, 6, c * P:c * P + P],
                                             v_st[:, pp, c * CH:c * CH + CH], eye[:])
                mm.then_inc(S["v_turned"], 1)

            def turn_probs(pp, p, first=False):
                pe.wait_ge(S["probs_ready"], p + 1)
                if not first:
                    pe.wait_ge(S["pt_copied"], p)
                for h in range(2):
                    for c in range(NCH):
                        mm = nc.tensor.transpose(ps[0:CH, 4 + h, c * P:c * P + P],
                                                 prob[:, pp, h, c * CH:c * CH + CH], eye[:])
                mm.then_inc(S["probs_turned"], 1)

            def mix(pp, p, first=False):
                pe.wait_ge(S["pt_copied"], p + 1)
                pe.wait_ge(S["vk_copied"], p + 1)
                if not first:
                    pe.wait_ge(S["mixed"], p)
                for c in range(NCH):
                    for h in range(2):
                        mm = nc.tensor.matmul(ps[C * h:C * h + C, 7, 0:P],
                                              v_key[0:CH, pp, c, C * h:C * h + C],
                                              prob_t[0:CH, pp, h, c, :],
                                              start=(c == 0), stop=(c == NCH - 1))
                mm.then_inc(S["pv_done"], 1)

            pe.wait_ge(S["c_loaded"], 16 * 6)
            scores(0, 0, 0, 0, early=True)
            scores(0, 0, 1, 1, early=True)
            turn_values(0, 0, first=True)
            turn_probs(0, 0, first=True)

            def rest_of_first(b2, hb):
                scores(b2, hb, 0, 2)
                turn_values(1, 1)
                mix(0, 0, first=True)
                turn_probs(1, 1)
                scores(b2, hb, 1, 3)
                turn_values(0, 2)
                mix(1, 1)

            rest_of_first(0, 1)
            with pe.Fori(2, 8) as r:
                b2 = pe.snap(r // 4)
                hb = pe.snap(r % 4)
                for xb in range(2):
                    p = 2 * r + xb - 2
                    turn_probs(xb, p)
                    scores(b2, hb, xb, p + 2)
                    turn_values(1 - xb, p + 1)
                    mix(xb, p)
            turn_probs(0, 14)
            turn_values(1, 15)
            mix(0, 14)
            turn_probs(1, 15)
            mix(1, 15)

            def turn_row(bank, src=h2):
                nc.tensor.transpose(ps[0:1, bank, 0:P], src[:, 0:1], eye[:]).then_inc(S["row_turned"], 1)

            pe.wait_ge(S["mixed"], NPAIR)
            turn_row(7, x2f)
            norm(x2f, 1)

            def attention(a, f, ev, row):
                pe.wait_ge(S["aw_loaded"], 16 * (a + 1))
                pe.sem_inc(S["passed"], 1)
                pe.wait_ge(S["section_done"], a + f + 1)
                pe.sem_inc(S["passed"], 1)
                for h in range(2):
                    nc.tensor.matmul(ps[C * h:C * h + C, 7, 0:C], wa[:, 0, :], wa[:, 1, :],
                                     start=True, stop=True)
                    mm = nc.tensor.matmul(ps[C * h:C * h + C, 5, 0:C], wa[:, 2, :], wa[:, 3, :],
                                          start=True, stop=True)
                mm.then_inc(S["fold_ready"], 1)
                base = pe.snap(NT * a)

                def queries(b2):
                    if b2 == 1:
                        pe.wait_ge(S["g_low"], 4 * a + 2)
                    for c in range(2):
                        s0 = b2 * NPOS + c * 512
                        mm = nc.tensor.matmul(ps[:, 6 + c, :], qk_bd[:], h2[:, s0:s0 + 512],
                                              start=True, stop=True)
                    mm.then_inc(S["g_ready"], 1)

                def values(b2):
                    bank = 4 + 2 * b2
                    if b2 == 1:
                        pe.wait_ge(S["g_low"], 4 * a + 4)
                    for c in range(NKC):
                        s0 = b2 * NPOS + c * P
                        mm = nc.tensor.matmul(ps[:, bank + c // 4, (c % 4) * P:(c % 4) * P + P],
                                              h2[:, s0:s0 + P], vo_bd[:], start=True, stop=True)
                    mm.then_inc(S["vo_ready"], 1)

                def tile_scores(n):
                    b2, q0, h = n // NTILE, (n % NTILE) // 2 * P, n % 2
                    if n % NTILE < 2:
                        pe.wait_ge(S["g_low"], 4 * a + 2 * b2 + h + 1)
                        pe.wait_ge(S["part_act"], 8 * a + 4 * b2 + 2 + 2 * h)
                    if n >= 2:
                        pe.wait_ge(S["s_exp"], base + n - 1)
                    for c in range(2):
                        for part in range(2):
                            mm = nc.tensor.matmul(ps[:, 2 * h + c, :], g_st[:, b2, h, q0:q0 + P],
                                                  h_st[:, b2, h, part, c * 512:c * 512 + 512],
                                                  start=(part == 0), stop=(part == 1))
                    mm.then_inc(S["s_ready"], 1)

                def tile_turn(n):
                    pe.wait_ge(S["s_prob"], base + n + 1)
                    if n == 0:
                        pe.wait_ge(S["vo_copied"], 2 * a + 1)
                    else:
                        pe.wait_ge(S["s_pt"], base + n)
                    for c in range(NKC):
                        mm = nc.tensor.transpose(ps[:, 4 + c // 4, (c % 4) * P:(c % 4) * P + P],
                                                 pr[:, n % 2, c * P:c * P + P], eye[:])
                    mm.then_inc(S["s_turned"], 1)

                def mix_chunk(g, c):
                    if c == 0:
                        pe.wait_ge(S["s_pt"], base + 8 * g + 8)
                        if g < 2:
                            pe.wait_ge(S["vo_copied"], 2 * a + 2)
                        else:
                            pe.wait_ge(S["a_stored"], 4 * a + g - 1)
                            if g == 2:
                                pe.wait_ge(S["decided"], a + f + 2)
                    for h in range(2):
                        mm = nc.tensor.matmul(ps[C * h:C * h + C, 6 + g % 2, :],
                                              vk[:, g // 2, c, C * h:C * h + C], prt[:, g % 2, h, c, :],
                                              start=(c == 0), stop=(c == NKC - 1))
                    if c == NKC - 1:
                        mm.then_inc(S["s_pv"], 1)

                pe.wait_ge(S["fold_a"], a + 1)
                queries(0)
                pe.wait_ge(S["fold_d"], a + 2)
                values(0)
                tile_scores(0)
                tile_scores(1)
                for n in range(NT):
                    if n + 2 < NT:
                        tile_scores(n + 2)
                    tile_turn(n)
                    if n == 0:
                        queries(1)
                    if n == 3:
                        values(1)
                    if n >= 8:
                        mix_chunk(n // 8 - 1, n % 8)
                    if n == 19:
                        pe.wait_ge(S["a_stored"], 4 * a + 1)
                        turn_row(6)
                for c in range(NKC):
                    mix_chunk(3, c)

            def feed_forward(a, f, ev, row):
                pe.wait_ge(S["w1_act"], f + 1)
                pe.wait_ge(S["w1_dve"], 2 * f + 2)

                def up(t):
                    b2, s0 = t // 2, t % 2 * 512
                    for h in range(2):
                        pe.wait_ge(S["f_act"], 16 * f + 4 * t + 3 + h)
                        if t > 0:
                            pe.wait_ge(S["relu_act"], 8 * f + 2 * t - 1 + h)
                            pe.wait_ge(S["relu_dve"], 8 * f + 2 * t - 1 + h)
                        for c in range(2):
                            for part in range(2):
                                mm = nc.tensor.matmul(ps[:, 2 * h + c, :], w1_st[:, c * P:c * P + P],
                                                      h_st[:, b2, h, part, s0:s0 + 512],
                                                      start=(part == 0), stop=(part == 1))
                        mm.then_inc(S["hid_ready"], 1)

                def down(t):
                    pe.wait_ge(S["relu_act"], 8 * f + 2 * t + 2)
                    pe.wait_ge(S["relu_dve"], 8 * f + 2 * t + 2)
                    src = hid if t % 2 == 0 else hid2
                    for c in range(2):
                        for h in range(2):
                            mm = nc.tensor.matmul(ps[C * h:C * h + C, 4 + t % 3, :],
                                                  w2p[:, c * C:c * C + C], src[:, 2 * h + c, :],
                                                  start=(c == 0), stop=(c == 1))
                    mm.then_inc(S["hid_down"], 1)

                up(0)
                up(1)
                down(0)
                up(2)
                down(1)
                pe.wait_ge(S["z_ready"], 4 * f + 1)
                turn_row(7)
                up(3)
                down(2)
                down(3)

            routed(pe, attention, feed_forward)

        @block.scalar
        def _(act):
            def load_table(func):
                nc.scalar.activation(spare[:, 0:1], eps_c[:, 0:1], func)

            def norm(k):
                for j in range(4):
                    act.wait_ge(S["centered"], 4 * k + j + 1)
                    nc.scalar.activation(sq[:, j * 512:j * 512 + 512], xc[:, j * 512:j * 512 + 512],
                                         ACT.Square).then_inc(S["squared"], 1)
                act.wait_ge(S["var_ready"], k + 1)
                nc.scalar.activation(sq[:, 0:256], ps[:, 4, 0:256], ACT.Sqrt,
                                     bias=eps_c[:, k:k + 1]).then_inc(S["std_ready"], 1)

            act.dma_start(x2[C:P], x_half[1]).then_inc(S["x_loaded"], 16)
            act.dma_start(spread_w[:], spread_mat).then_inc(S["s_loaded"], 16)
            act.dma_start(wq_nat[:], w_q).then_inc(S["w_loaded"], 16)
            act.dma_start(rel_tab[:], bias_tables).then_inc(S["w_loaded"], 16)
            act.dma_start(masks8[:, 0, :], attn_mask).then_inc(S["m_loaded"], 16)
            act.dma_start(masks8[:, 1, :], ffn_mask).then_inc(S["m_loaded"], 16)
            act.dma_start(iota[:], iotas).then_inc(S["m_loaded"], 16)
            act.dma_start(eye[:], ident).then_inc(S["c_loaded"], 16)
            act.wait_ge(S["eps_set"], 1)
            load_table(ACT.Sqrt)
            norm(0)
            act.wait_ge(S["zeroed"], 1)
            for h in range(2):
                act.wait_ge(S["tab_ready"], 1)
                for tab, at, n in ((gx, 0, KC), (gy, TX, KR)):
                    src = ps[C * h:C * h + C, 7, at:at + 1]
                    shifted = bass.AP(tensor=src.tensor, offset=src.offset,
                                      ap=[list(src.ap[0]), [1, n], [1, 32]])
                    nc.scalar.copy(tab[C * h:C * h + C, :, h, :], shifted
                                   ).then_inc(S["tab_copied"], 1)
            for j in range(4):
                act.wait_ge(S["v_ready"], j + 1)
                r0 = PAD + 16 * (j % 2)
                nc.scalar.copy(v_pad[:, j // 2, r0:r0 + 16, PAD:PAD + WW],
                               ps[:, VBANK[j], :].rearrange("p (r w) -> p r w", w=WW)
                               ).then_inc(S["v_copied"], 1)
            for j in range(4):
                for h in range(2):
                    act.wait_ge(S["qk_ready"], 2 * j + h + 1)
                    nc.scalar.copy(q_aug[0:C, 2 * h + j // 2, 16 * (j % 2):16 * (j % 2) + 16, :],
                                   ps[0:C, QKBANK[2 * j + h], :].rearrange("p (r w) -> p r w", w=WW)
                                   ).then_inc(S["q_copied"], 1)
            def exps(pp, p, early=False):
                act.wait_ge(S["negmax_ready"], p + 1)
                if not early:
                    act.wait_ge(S["probs_turned"], p - 1)
                for h in range(2):
                    ins = nc.scalar.activation(prob[:, pp, h, 0:NKEY], ps[:, 2 * pp + h, 0:NKEY],
                                               ACT.Exp, bias=negmax[:, pp, h:h + 1],
                                               accum_out=rowsum[:, pp, h:h + 1])
                ins.then_inc(S["exp_done"], 1)

            def copy_turned(pp, p, early=False):
                act.wait_ge(S["probs_turned"], p + 1)
                if not early:
                    act.wait_ge(S["pv_done"], p - 1)
                for h in range(2):
                    ins = nc.scalar.copy(prob_t[0:CH, pp, h, :, :],
                                         ps[0:CH, 4 + h, 0:NCH * P].rearrange("p (c q) -> p c q", c=NCH))
                ins.then_inc(S["pt_copied"], 1)

            exps(0, 0, early=True)
            exps(1, 1, early=True)
            for pp in range(2):
                copy_turned(pp, pp, early=True)
                exps(pp, pp + 2)
            with act.Fori(1, 7) as r:
                for pp in range(2):
                    copy_turned(pp, 2 * r + pp)
                    exps(pp, 2 * r + pp + 2)
            for pp in range(2):
                copy_turned(pp, 14 + pp)

            load_table(ACT.Sqrt)
            norm(1)
            load_table(ACT.Exp)

            def attention(a, f, ev, row):
                base = act.snap(NT * a)

                def high(b2, h):
                    rows = slice(C * h, C * h + C)
                    nc.scalar.copy(h_st[rows, b2, h, 0, :], h2[rows, b2 * NPOS:b2 * NPOS + NPOS]
                                   ).then_inc(S["part_act"], 1)

                def low(b2, h):
                    act.wait_ge(S["part_dve"], 8 * a + 4 * b2 + 2 + 2 * h)
                    nc.scalar.copy(h_st[C * (1 - h):C * (1 - h) + C, b2, h, 1, :],
                                   h_f[C * h:C * h + C, b2, h, 1, :]).then_inc(S["part_act"], 1)

                def query_high(b2, h):
                    act.wait_ge(S["g_ready"], 2 * a + b2 + 1)
                    nc.scalar.copy(g_st[C * h:C * h + C, b2, h, :], ps[C * h:C * h + C, 6:8, :]
                                   ).then_inc(S["g_high"], 1)

                def copy_values(b2):
                    act.wait_ge(S["vo_ready"], 2 * a + b2 + 1)
                    nc.scalar.copy(vk[:, b2, :, :],
                                   ps[:, 4 + 2 * b2:6 + 2 * b2, :].rearrange("p b (c d) -> p (b c) d", c=4)
                                   ).then_inc(S["vo_copied"], 1)

                def exps(n):
                    act.wait_ge(S["s_negmax"], base + n + 1)
                    if n >= 2:
                        act.wait_ge(S["s_turned"], base + n - 1)
                    nc.scalar.activation(pr[:, n % 2, :], ps[:, 2 * (n % 2):2 * (n % 2) + 2, :],
                                         ACT.Exp, bias=negmax[:, 0, n % 2:n % 2 + 1],
                                         accum_out=rowsum[:, 0, n % 2:n % 2 + 1]
                                         ).then_inc(S["s_exp"], 1)

                act.wait_ge(S["section_done"], a + f + 1)
                act.wait_ge(S["fold_ready"], a + 1)
                for h in range(2):
                    ins = nc.scalar.mul(qk_bd[C * h:C * h + C, C * h:C * h + C],
                                        ps[C * h:C * h + C, 7, 0:C], SCALE)
                ins.then_inc(S["fold_a"], 1)
                high(0, 0)
                query_high(0, 0)
                low(0, 0)
                high(0, 1)
                query_high(0, 1)
                low(0, 1)
                exps(0)
                copy_values(0)
                between = {1: lambda: query_high(1, 0), 2: lambda: query_high(1, 1),
                           3: lambda: high(1, 0), 5: lambda: copy_values(1), 6: lambda: low(1, 0),
                           7: lambda: high(1, 1), 9: lambda: low(1, 1)}
                for n in range(NT):
                    if n + 1 < NT:
                        exps(n + 1)
                    act.wait_ge(S["s_turned"], base + n + 1)
                    if n % 8 == 0 and n >= 16:
                        act.wait_ge(S["s_pv"], 4 * a + n // 8 - 1)
                    q0 = (n // 2 % 4) * P
                    nc.scalar.copy(prt[:, n // 8 % 2, n % 2, :, q0:q0 + P],
                                   ps[:, 4:6, :].rearrange("p b (c q) -> p (b c) q", c=4)
                                   ).then_inc(S["s_pt"], 1)
                    if n in between:
                        between[n]()

            def feed_forward(a, f, ev, row):
                act.wait_ge(S["fw_loaded"], 48 * (f + 1))
                act.wait_ge(S["section_done"], a + f + 1)
                nc.scalar.copy(w1_st[0:C, :], w1d[0:C, :]).then_inc(S["w1_act"], 1)

                def high(t, h):
                    rows = slice(C * h, C * h + C)
                    nc.scalar.copy(h_st[rows, t // 2, h, 0, t % 2 * 512:t % 2 * 512 + 512],
                                   h2[rows, t * 512:t * 512 + 512]).then_inc(S["f_act"], 1)

                def low(t, h):
                    act.wait_ge(S["f_dve"], 16 * f + 4 * t + 2 + 2 * h)
                    s = slice(t % 2 * 512, t % 2 * 512 + 512)
                    nc.scalar.copy(h_st[C * (1 - h):C * (1 - h) + C, t // 2, h, 1, s],
                                   h_f[C * h:C * h + C, t // 2, h, 1, s]).then_inc(S["f_act"], 1)

                def relu(t, h):
                    dst = hid if t % 2 == 0 else hid2
                    act.wait_ge(S["hid_ready"], 8 * f + 2 * t + h + 1)
                    if t >= 2:
                        act.wait_ge(S["hid_down"], 4 * f + t - 1)
                    nc.scalar.activation(dst[:, 2 * h, :], ps[:, 2 * h, :], ACT.Relu,
                                         bias=w2p[:, 2 * C:2 * C + 1]).then_inc(S["relu_act"], 1)

                high(0, 0)
                high(0, 1)
                low(0, 0)
                low(0, 1)
                for t in range(4):
                    if t < 3:
                        high(t + 1, 0)
                        high(t + 1, 1)
                    relu(t, 0)
                    if t < 3:
                        low(t + 1, 0)
                    relu(t, 1)
                    if t < 3:
                        low(t + 1, 1)

            routed(act, attention, feed_forward)
            store_output(act, 1)

        @block.vector
        def _(dve):
            nc.vector.memset(eps_c[:, 0:1], LN_C_EPS)
            nc.vector.memset(eps_c[:, 1:2], LN_T_EPS).then_inc(S["eps_set"], 1)
            dve.sem_inc(S["fold_d"], 1)
            dve.sem_inc(S["ffn_done"], 1)
            dve.wait_ge(S["x_loaded"], 48)

            def make_table():
                steps = [0]

                def step(ins):
                    steps[0] += 1
                    ins.then_inc(S["dve_step"], 1)
                    dve.wait_ge(S["dve_step"], steps[0])

                dve.wait_ge(S["m_loaded"], 48)
                step(nc.vector.memset(ahead[:], 4.0 * NB))
                step(nc.vector.tensor_copy(kinds[:], masks8[:]))
                step(nc.vector.scalar_tensor_tensor(kinds[:, 0, :], kinds[:, 1, :], 2.0, kinds[:, 0, :],
                                                    ALU.mult, ALU.add))
                step(nc.vector.tensor_scalar(kinds[:, 1, :], kinds[:, 0, :], 0.0, 4.0 * NB,
                                             ALU.is_equal, ALU.mult))
                step(nc.vector.tensor_tensor(kinds[:, 0, :], kinds[:, 0, :], iota[:], ALU.add))
                step(nc.vector.tensor_tensor(ahead[:, 0, 0:NB], kinds[:, 0, :], kinds[:, 1, :], ALU.max))
                by, at = 1, 0
                while by < NB:
                    step(nc.vector.tensor_tensor(ahead[:, 1 - at, 0:NB], ahead[:, at, 0:NB],
                                                 ahead[:, at, by:by + NB], ALU.min))
                    by, at = 2 * by, 1 - at
                nc.vector.tensor_copy(ahead_i[:], ahead[:, at, 0:NB + 1]).then_inc(S["table_ready"], 1)

            def norm(src, k, between=None):
                for j in range(4):
                    s = slice(j * 512, j * 512 + 512)
                    dve.wait_ge(S["mean_ready"], 4 * k + j + 1)
                    nc.vector.tensor_tensor(xc[:, s], src[:, s], ps[:, j, :], ALU.subtract
                                            ).then_inc(S["centered"], 1)
                if between is not None:
                    between()
                dve.wait_ge(S["std_ready"], k + 1)
                nc.vector.reciprocal(sq[:, 0:256], sq[:, 0:256]).then_inc(S["inv_ready"], 1)
                for j in range(4):
                    s = slice(j * 512, j * 512 + 512)
                    dve.wait_ge(S["spread_ready"], 4 * k + j + 1)
                    nc.vector.tensor_tensor(h2[:, s], xc[:, s], ps[:, j, :], ALU.mult
                                            ).then_inc(S["normed"], 1)

            norm(x2f, 0, make_table)
            dve.wait_ge(S["zeroed"], 1)
            for j in range(4):
                for h in range(2):
                    dve.wait_ge(S["qk_ready"], 2 * j + h + 1)
                    r0 = PAD + 16 * (j % 2)
                    nc.vector.tensor_copy(k_aug[0:C, 2 * h + j // 2, r0:r0 + 16, PAD:PAD + WW],
                                          ps[C:P, QKBANK[2 * j + h], :].rearrange("p (r w) -> p r w", w=WW)
                                          ).then_inc(S["k_copied"], 1)
            dve.wait_ge(S["c_loaded"], 16 * 6)
            for k in range(8):
                dve.wait_ge(S["bias_ready"], k + 1)
                for h in range(2):
                    rows = slice(32 * h, 32 * h + 32)
                    if k < 4:
                        bank, dst0 = QKBANK[k], XROW
                        dst = q_aug[dst0:dst0 + 32, 2 * h:2 * h + 2, :, 8 * k:8 * k + 8].rearrange(
                            "p a r w -> p w a r")
                        got = ps[rows, bank, :].rearrange("p (w a r) -> p w a r", w=8, a=2)
                        mask = mask_x[rows, 8 * k:8 * k + 8]
                        shape = [32, 8, 2, HH]
                    else:
                        bank, r0, dst0 = QKBANK[k], 8 * (k - 4), YROW
                        dst = q_aug[dst0:dst0 + 32, 2 * h:2 * h + 2, r0:r0 + 8, :].rearrange(
                            "p a r w -> p r a w")
                        got = ps[rows, bank, :].rearrange("p (r a w) -> p r a w", r=8, a=2)
                        mask = mask_x[rows, WW + r0:WW + r0 + 8]
                        shape = [32, 8, 2, WW]
                    nc.vector.tensor_tensor(dst, got, mask.unsqueeze(2).unsqueeze(3).broadcast_to(shape),
                                            ALU.add).then_inc(S["bias_added"], 1)

            def maxima(pp, p):
                dve.wait_ge(S["scores_ready"], p + 1)
                nc.vector.tensor_reduce(negmax[:, pp, :], ps[:, 2 * pp:2 * pp + 2, 0:NKEY], X, ALU.max,
                                        negate=True).then_inc(S["negmax_ready"], 1)

            def normalise(pp, p):
                dve.wait_ge(S["exp_done"], p + 1)
                nc.vector.reciprocal(rinv[:, pp, :], rowsum[:, pp, :]).then_inc(S["rinv_ready"], 1)
                dve.wait_ge(S["rinv_ready"], p + 1)
                for h in range(2):
                    ins = nc.vector.tensor_scalar(prob[:, pp, h, 0:NKEY], prob[:, pp, h, 0:NKEY],
                                                  rinv[:, pp, h:h + 1], None, ALU.mult)
                ins.then_inc(S["probs_ready"], 1)

            def copy_values(pp, p, early=False):
                dve.wait_ge(S["v_turned"], p + 1)
                if not early:
                    dve.wait_ge(S["pv_done"], p - 1)
                nc.vector.tensor_copy(v_key[0:CH, pp, :, :],
                                      ps[0:CH, 6, 0:NCH * P].rearrange("p (c d) -> p c d", c=NCH)
                                      ).then_inc(S["vk_copied"], 1)

            def add_mixed(b2, hb, xb, p):
                dve.wait_ge(S["pv_done"], p + 1)
                win = x2[:, bass.ds(b2, 1), bass.ds(BR * hb, BR), BC * xb:BC * xb + BC]
                nc.vector.tensor_tensor(win, win,
                                        ps[:, 7, 0:P].rearrange("p (a r c) -> p a r c", a=1, c=BC),
                                        ALU.add).then_inc(S["mixed"], 1)

            maxima(0, 0)
            maxima(1, 1)
            normalise(0, 0)
            copy_values(0, 0, early=True)
            normalise(1, 1)
            maxima(0, 2)
            copy_values(1, 1, early=True)
            add_mixed(0, 0, 0, 0)
            normalise(0, 2)
            maxima(1, 3)
            copy_values(0, 2)
            add_mixed(0, 0, 1, 1)
            with dve.Fori(1, 7) as r:
                b2 = dve.snap(r // 4)
                hb = dve.snap(r % 4)
                for xb in range(2):
                    p = 2 * r + xb
                    normalise(1 - xb, p + 1)
                    maxima(xb, p + 2)
                    copy_values(1 - xb, p + 1)
                    add_mixed(b2, hb, xb, p)
            normalise(1, 15)
            copy_values(1, 15)
            add_mixed(1, 3, 0, 14)
            add_mixed(1, 3, 1, 15)
            dve.wait_ge(S["mixed"], NPAIR)

            def decide(n, ev=None):
                dve.wait_ge(S["row_turned"], n + 1)
                if ev is not None:
                    dve.wait_ge(S["info_read"], readers * ev + readers)
                dve.sem_inc(S["passed"], 1)
                bank = 7 if ev is None else decide.bank
                nc.vector.max(top8[:], ps[0:1, bank, 0:NOPS]).then_inc(S["op_max"], 1)
                dve.wait_ge(S["op_max"], n + 1)
                dve.sem_inc(S["passed"], 1)
                nc.vector.max_index(idx8[:], top8[:], ps[0:1, bank, 0:NOPS]).then_inc(S["decided"], 1)

            decide(0)
            norm(x2f, 1)
            dve.wait_ge(S["normed"], 8)
            dve.sem_inc(S["section_done"], 1)

            def attention(a, f, ev, row):
                base = dve.snap(NT * a)

                def high(b2, h):
                    nc.vector.tensor_copy(h_st[C * (1 - h):C * (1 - h) + C, b2, h, 0, :],
                                          h2[C * h:C * h + C, b2 * NPOS:b2 * NPOS + NPOS]
                                          ).then_inc(S["part_dve"], 1)

                def low(b2, h):
                    dve.wait_ge(S["part_act"], 8 * a + 4 * b2 + 1 + 2 * h)
                    rows = slice(C * h, C * h + C)
                    nc.vector.tensor_tensor(h_st[rows, b2, h, 1, :], h2[rows, b2 * NPOS:b2 * NPOS + NPOS],
                                            h_f[rows, b2, h, 0, :], ALU.subtract
                                            ).then_inc(S["part_dve"], 1)

                def query_low(b2, h):
                    dve.wait_ge(S["g_high"], 4 * a + 2 * b2 + h + 1)
                    nc.vector.tensor_tensor(g_st[C * (1 - h):C * (1 - h) + C, b2, h, :],
                                            ps[C * h:C * h + C, 6:8, :],
                                            g_f[C * h:C * h + C, b2, h, :], ALU.subtract
                                            ).then_inc(S["g_low"], 1)

                def maxima(n):
                    dve.wait_ge(S["s_ready"], base + n + 1)
                    nc.vector.tensor_reduce(negmax[:, 0, n % 2:n % 2 + 1],
                                            ps[:, 2 * (n % 2):2 * (n % 2) + 2, :],
                                            mybir.AxisListType.XY, ALU.max, negate=True
                                            ).then_inc(S["s_negmax"], 1)

                def normalise(n):
                    dve.wait_ge(S["s_exp"], base + n + 1)
                    nc.vector.reciprocal(rinv[:, 0, n % 2:n % 2 + 1], rowsum[:, 0, n % 2:n % 2 + 1]
                                         ).then_inc(S["s_rinv"], 1)
                    dve.wait_ge(S["s_rinv"], base + n + 1)
                    nc.vector.tensor_scalar(pr[:, n % 2, :], pr[:, n % 2, :],
                                            rinv[:, 0, n % 2:n % 2 + 1], None, ALU.mult
                                            ).then_inc(S["s_prob"], 1)

                def store(g):
                    dve.wait_ge(S["s_pv"], 4 * a + g + 1)
                    nc.vector.tensor_copy(h2[:, g * 512:g * 512 + 512], ps[:, 6 + g % 2, :]
                                          ).then_inc(S["a_stored"], 1)

                dve.wait_ge(S["fold_ready"], a + 1)
                for h in range(2):
                    ins = nc.vector.tensor_copy(vo_bd[C * h:C * h + C, C * h:C * h + C],
                                                ps[C * h:C * h + C, 5, 0:C])
                ins.then_inc(S["fold_d"], 1)
                high(0, 0)
                low(0, 0)
                query_low(0, 0)
                high(0, 1)
                low(0, 1)
                maxima(0)
                query_low(0, 1)
                maxima(1)
                between = {2: lambda: query_low(1, 0), 3: lambda: query_low(1, 1),
                           4: lambda: high(1, 0), 5: lambda: low(1, 0),
                           6: lambda: high(1, 1), 8: lambda: low(1, 1)}
                for n in range(NT):
                    normalise(n)
                    if n + 2 < NT:
                        maxima(n + 2)
                    if n in between:
                        between[n]()
                    if n == 17:
                        store(0)
                    if n == 20:
                        decide.bank = 6
                        decide(a + f + 1, ev)
                    if n == 25:
                        store(1)
                store(2)
                store(3)
                dve.wait_ge(S["a_stored"], 4 * a + 4)
                dve.sem_inc(S["section_done"], 1)

            def feed_forward(a, f, ev, row):
                dve.wait_ge(S["fw_loaded"], 48 * (f + 1))
                nc.vector.tensor_copy(w1_hi[C:P, :], w1d[C:P, :]).then_inc(S["w1_dve"], 1)
                dve.wait_ge(S["w1_dve"], 2 * f + 1)
                nc.vector.tensor_tensor(w1_st[C:P, :], w1d[C:P, :], w1_hi[C:P, :].bitcast(F32),
                                        ALU.subtract).then_inc(S["w1_dve"], 1)

                def parts(t, h):
                    rows = slice(C * h, C * h + C)
                    s, cols = slice(t % 2 * 512, t % 2 * 512 + 512), slice(t * 512, t * 512 + 512)
                    nc.vector.tensor_copy(h_st[C * (1 - h):C * (1 - h) + C, t // 2, h, 0, s],
                                          h2[rows, cols]).then_inc(S["f_dve"], 1)
                    dve.wait_ge(S["f_act"], 16 * f + 4 * t + 1 + h)
                    nc.vector.tensor_tensor(h_st[rows, t // 2, h, 1, s], h2[rows, cols],
                                            h_f[rows, t // 2, h, 0, s], ALU.subtract
                                            ).then_inc(S["f_dve"], 1)

                def relu(t, h):
                    dst = hid if t % 2 == 0 else hid2
                    dve.wait_ge(S["hid_ready"], 8 * f + 2 * t + h + 1)
                    nc.vector.tensor_scalar(dst[:, 2 * h + 1, :], ps[:, 2 * h + 1, :],
                                            w2p[:, 2 * C + 1:2 * C + 2], 0.0, ALU.add, ALU.max
                                            ).then_inc(S["relu_dve"], 1)

                def store(t):
                    dve.wait_ge(S["hid_down"], 4 * f + t + 1)
                    nc.vector.tensor_scalar(h2[:, t * 512:t * 512 + 512], ps[:, 4 + t % 3, :],
                                            w2p[:, 2 * C + 2:2 * C + 3], None, ALU.add
                                            ).then_inc(S["z_ready"], 1)

                parts(0, 0)
                parts(0, 1)
                for t in range(4):
                    if t < 3:
                        parts(t + 1, 0)
                    relu(t, 0)
                    if t < 3:
                        parts(t + 1, 1)
                    relu(t, 1)
                    if t > 0:
                        store(t - 1)
                    if t == 2:
                        decide.bank = 7
                        decide(a + f + 1, ev)
                store(3)
                dve.wait_ge(S["z_ready"], 4 * f + 4)
                dve.sem_inc(S["ffn_done"], 1)
                dve.sem_inc(S["section_done"], 1)

            routed(dve, attention, feed_forward)
            for j in range(4):
                s = slice(j * 512, j * 512 + 512)
                nc.vector.tensor_tensor(xc[:, s], x2f[:, s], h2[:, s], ALU.add
                                        ).then_inc(S["out_ready"], 1)


def constants():
    import numpy as np

    key_onehot = np.zeros((C, HP, WP), np.float32)
    for r in range(KC):
        key_onehot[r, :, r::KC] = 1.0
    for r in range(KR):
        key_onehot[YROW - XROW + r, r::KR, :] = 1.0
    masks = np.zeros((P, WW + HH), np.float32)
    for h in range(2):
        for r in range(KC):
            for w in range(WW):
                masks[32 * h + r, w] = 0.0 if (r - w) % KC < KS else -1e30
        for r in range(KR):
            for y in range(HH):
                masks[32 * h + r, WW + y] = 0.0 if (r - y) % KR < KS else -1e30
    ident = np.eye(P, dtype=np.float32)
    mean_mat = np.zeros((P, P + 2 * 32), np.float32)
    spread_mat = np.zeros((P, 8, P), np.float32)
    for h in range(2):
        rows = slice(C * h, C * h + C)
        mean_mat[rows, rows] = 1.0 / C
        for slot in range(2):
            at = P + 32 * slot + 16 * slot + 8 * h
            mean_mat[rows, at:at + 8] = 1.0 / C
            for j in range(4):
                spread_mat[32 * j + 16 * slot + 8 * h, 2 * j + slot, rows] = 1.0
    iotas = np.tile(4.0 * np.arange(NB, dtype=np.float32), (NOPS, 1))
    return key_onehot, masks, ident, mean_mat, spread_mat, iotas


def kernel(x, L0_conv_wq, L0_conv_wk, L0_conv_wv, L0_conv_rel_x, L0_conv_rel_y,
           L0_ffn_ffn_w1, L0_ffn_ffn_b1, L0_ffn_ffn_w2, L0_ffn_ffn_b2,
           L0_ffn_wq, L0_ffn_wk, L0_ffn_wv, L0_ffn_wo, L0_ffn_attn_mask, L0_ffn_ffn_mask):
    import numpy as np
    import concourse.bacc as bacc
    from concourse.bass_utils import run_bass_kernel_spmd

    x = np.ascontiguousarray(x)
    wq, wk, wv = (np.asarray(w) for w in (L0_conv_wq, L0_conv_wk, L0_conv_wv))
    rel_x, rel_y = np.asarray(L0_conv_rel_x), np.asarray(L0_conv_rel_y)
    tables = np.zeros((C, TX + TY), np.float32)
    half = rel_x.shape[0]
    for c in range(C):
        d = c % (2 * half)
        table, rel, period, length, at = ((0, rel_x, KC, TX, 0) if d < half else (1, rel_y, KR, TY, TX))
        for t in range(length):
            if t % period < KS:
                tables[c, at + t] = rel[d % half, t % period]
    n = NB * NOPS
    flat = lambda w: np.asarray(w).reshape((n,) + np.asarray(w).shape[2:])
    turned = lambda w: flat(w).transpose(0, 2, 1)
    attn_pack = np.ascontiguousarray(np.stack(
        [turned(L0_ffn_wq), turned(L0_ffn_wk), turned(L0_ffn_wv), flat(L0_ffn_wo)], axis=2))
    w2 = flat(L0_ffn_ffn_w2).reshape(n, 2, P, C).transpose(0, 2, 1, 3).reshape(n, P, 2 * C)
    b1 = flat(L0_ffn_ffn_b1).reshape(n, 2, P).transpose(0, 2, 1)
    b2 = np.concatenate([flat(L0_ffn_ffn_b2)] * 2, axis=1)[:, :, None]
    ffn_pack = np.ascontiguousarray(np.concatenate([w2, b1, b2], axis=2))
    key_onehot, masks, ident, mean_mat, spread_mat, iotas = constants()
    arrays = {
        "x": x,
        "w_qk": np.ascontiguousarray(np.concatenate([wq.T, wk.T], axis=1)),
        "w_q": np.ascontiguousarray(wq),
        "w_v": np.ascontiguousarray(wv.T),
        "bias_tables": tables,
        "key_onehot": key_onehot, "masks": masks, "ident": ident, "mean_mat": mean_mat, "spread_mat": spread_mat,
        "iotas": iotas,
        "attn_mask": np.ascontiguousarray(np.asarray(L0_ffn_attn_mask).T),
        "ffn_mask": np.ascontiguousarray(np.asarray(L0_ffn_ffn_mask).T),
        "attn_pack": attn_pack,
        "ffn_w1": np.ascontiguousarray(flat(L0_ffn_ffn_w1)),
        "ffn_pack": ffn_pack,
    }
    nc = bacc.Bacc("TRN2", target_bir_lowering=False, num_devices=1)
    handles = {k: nc.dram_tensor(f"in_{k}", a.shape, mybir.dt.from_np(a.dtype), kind="ExternalInput").ap()
               for k, a in arrays.items()}
    out = nc.dram_tensor("out", x.shape, F32, kind="ExternalOutput").ap()
    build(nc, out=out, **handles)
    r = run_bass_kernel_spmd(nc, [{f"in_{k}": a for k, a in arrays.items()}], core_ids=[0])
    return r.results[0]["out"]
```

```python
from contextlib import ExitStack

import concourse.bass as bass
from concourse import mybir

F32 = mybir.dt.float32
F32R = mybir.dt.float32r
I32 = mybir.dt.int32
U32 = mybir.dt.uint32
U8 = mybir.dt.uint8
ALU = mybir.AluOpType
ACT = mybir.ActivationFunctionType
X = mybir.AxisListType.X

P = 128
C = 64
HH, WW = 32, 32
NPOS = HH * WW
COLS = 2 * NPOS
KS, PAD = 7, 3
HP, WP = HH + 2 * PAD, WW + 2 * PAD
BR, BC = 8, 16
KR, KC = BR + KS - 1, BC + KS - 1
NKEY = KR * KC
NCH, CH = 3, 103
NPAIR = 16
XROW, YROW = 64, 96
TX, TY = 32 + KC - 1, 32 + KR - 1
NB, NOPS, HID = 33, 19, 256
NTILE = 16
NT = 2 * NTILE
NKC = NPOS // P
SCALE = float(C) ** -0.5
LN_C_EPS, LN_T_EPS = 1e-6, 1e-5
VBANK, QKBANK = (4, 5, 6, 0), (1, 2, 3, 7, 4, 5, 6, 0)
GBANK = (2, 6, 7, 6)
BBANK = (1, 4, 6, 7)
W2COLS = 2 * C + 2 + 1


def build(nc, x, w_qk, w_q, w_v, bias_tables, key_onehot, masks, ident, mean_mat, spread_mat, iotas,
          attn_mask, ffn_mask, attn_pack, ffn_w1, ffn_pack, out):
    with ExitStack() as ctx:
        def sb(name, shape, dt=F32):
            return ctx.enter_context(nc.sbuf_tensor(name, shape, dt))

        def sem(name):
            return ctx.enter_context(nc.semaphore(name))

        ps = ctx.enter_context(nc.psum_tensor("ps", [P, 8, 512], F32))

        eye = sb("eye", [P, P])
        mean_w = sb("mean_w", [P, P + 2 * 32])
        spread_w = sb("spread_w", [P, 8, P])
        masks_xy = sb("masks_xy", [P, WW])
        wqk = sb("wqk", [P, 2, P])
        wq_nat = sb("wq_nat", [C, C])
        wv_bd = sb("wv_bd", [P, P])
        rel_tab = sb("rel_tab", [C, TX + TY])
        tabs = sb("tabs", [P, (KC + KR) * 2 * 32])
        gx = tabs[:, 0:KC * 64].rearrange("p (s a r) -> p s a r", a=2, r=32)
        gy = tabs[:, KC * 64:(KC + KR) * 64].rearrange("p (s a r) -> p s a r", a=2, r=32)
        osum = tabs[:, 0:COLS]
        eps_c = sb("eps_c", [P, 2])
        ones_c = sb("ones_c", [P, 1])
        spare = sb("spare", [P, 1])
        x2 = sb("x2", [P, 2, HH, WW])
        xc = sb("xc", [P, COLS])
        sq = sb("sq", [P, COLS])
        h2 = sb("h2", [P, COLS])
        arena = sb("arena", [P, 2 * 2 * NKC * 512])
        n_q, n_k, n_v = 4 * NPOS, 4 * HP * WP, 2 * HP * WP
        q_aug = arena[:, 0:n_q].rearrange("p (a h w) -> p a h w", a=4, w=WW)
        k_aug = arena[:, n_q:n_q + n_k].rearrange("p (a h w) -> p a h w", a=4, w=WP)
        v_pad = arena[:, n_q + n_k:n_q + n_k + n_v].rearrange("p (a h w) -> p a h w", a=2, w=WP)
        prt = arena.rearrange("p (a b c q) -> p a b c q", a=2, b=2, c=NKC)
        q_st = sb("q_st", [P, 2, 2, BR * BC])
        v_st = sb("v_st", [P, 2, NCH * CH])
        v_key = sb("v_key", [P, 2, NCH, P])
        prob = sb("prob", [P, 2, 2, NCH * CH])
        prob_t = sb("prob_t", [P, 2, 2, NCH, P])
        negmax = sb("negmax", [P, 2, 2])
        rowsum = sb("rowsum", [P, 2, 2])
        rinv = sb("rinv", [P, 2, 2])
        masks8 = sb("masks8", [NOPS, 2, NB], U8)
        kinds = sb("kinds", [NOPS, 2, NB])
        iota = sb("iota", [NOPS, NB])
        ahead = sb("ahead", [NOPS, 2, 2 * NB])
        ahead_i = sb("ahead_i", [NOPS, NB + 1], I32)
        table = sb("table", [1, NOPS * (NB + 1)], I32)
        top8 = sb("top8", [1, 8])
        idx8 = sb("idx8", [1, 8], U32)
        wa = sb("wa", [C, 4, C])
        qk_bd = sb("qk_bd", [P, P])
        vo_bd = sb("vo_bd", [P, P])
        h_st = sb("h_st", [P, 2, 2, 2, NPOS], F32R)
        g_st = sb("g_st", [P, 2, 2, NPOS], F32R)
        h_f, g_f = h_st.bitcast(F32), g_st.bitcast(F32)
        vk = sb("vk", [P, 2, NKC, P])
        pr = sb("pr", [P, 2, NPOS])
        w1d = sb("w1d", [P, HID])
        w1_hi = sb("w1_hi", [P, HID], F32R)
        w1_st = sb("w1_st", [P, HID], F32R)
        w2p = sb("w2p", [P, W2COLS])
        hid = xc.rearrange("p (a b) -> p a b", a=4)
        hid2 = sq.rearrange("p (a b) -> p a b", a=4)

        next_steps = nc.dram_tensor("next_steps", (NOPS, NB + 1), I32, kind="Internal").ap()

        names = """x_loaded w_loaded c_loaded m_loaded s_loaded zeroed w_zeroed eps_set
            mean_ready centered squared var_ready std_ready rstd_ready normed
            tab_ready tab_copied qk_ready q_copied k_copied v_ready v_copied bias_ready bias_added
            q_staged v_staged scores_ready negmax_ready exp_done rinv_ready probs_ready
            probs_turned pt_copied v_turned vk_copied pv_done mixed spread_ready
            row_turned dve_step op_max decided passed info_read section_done ffn_done
            table_ready table_spilled table_loaded inv_ready
            aw_loaded fw_loaded fold_ready fold_a fold_d
            g_ready g_high g_low vo_ready vo_copied
            s_ready s_negmax s_exp s_rinv s_prob s_turned s_pt s_pv a_stored
            w1_act w1_dve high_low_act high_low_dve hid_ready relu_act relu_dve hid_down z_ready
            summed stored""".split()
        S = {n: sem(n) for n in names}

        x_half = [x[2 * h:2 * h + 2].rearrange("b c r w -> c b r w") for h in range(2)]
        o_half = [out[2 * h:2 * h + 2].rearrange("b c r w -> c b (r w)") for h in range(2)]
        x2f = x2.rearrange("p a h w -> p (a h w)")

        block = ctx.enter_context(nc.Block())

        readers = 5

        def routing(eng):
            name = eng.engine.name
            op, entry, step, cur, last, stride, am, fm, n_att, n_ffn, event = (
                eng.alloc_register(f"{name}_{k}")
                for k in "op entry step cur last stride am fm n_att n_ffn event".split())
            for reg in (n_att, n_ffn, event, cur):
                eng.reg_mov(reg, 0)

            def sections():
                return eng.snap(n_att, min_val=0, max_val=NB) + eng.snap(n_ffn, min_val=0, max_val=NB)

            def load_next():
                eng.wait_ge(S["table_loaded"], 16)
                eng.wait_ge(S["decided"], sections() + 1)
                eng.sem_inc(S["passed"], 1)
                eng.load(op, idx8[0:1, 0:1])
                at = (eng.snap(op, min_val=0, max_val=NOPS - 1) * (NB + 1)
                      + eng.snap(cur, min_val=0, max_val=NB))
                eng.load(entry, table[0:1, bass.ds(at, 1)])
                eng.sem_inc(S["info_read"], 1)
                eng.reg_alu(step, entry, 2, op=ALU.arith_shift_right)
                eng.reg_alu(am, entry, 1, op=ALU.bitwise_and)
                eng.reg_alu(fm, entry, 2, op=ALU.bitwise_and)
                eng.reg_add(cur, step, 1)
                eng.reg_alu(cur, cur, NB, op=ALU.min)

            def run_event(attention, feed_forward):
                def section(mask, work, done):
                    with eng.If(eng.snap(mask, min_val=0, max_val=2) > 0):
                        work(eng.snap(n_att, min_val=0, max_val=NB),
                             eng.snap(n_ffn, min_val=0, max_val=NB),
                             eng.snap(event, min_val=0, max_val=NB),
                             eng.snap(eng.snap(step, min_val=0, max_val=NB - 1) * NOPS
                                      + eng.snap(op, min_val=0, max_val=NOPS - 1)))
                        eng.reg_add(done, done, 1)

                section(am, attention, n_att)
                section(fm, feed_forward, n_ffn)
                eng.reg_add(event, event, 1)
                load_next()

            def run(attention, feed_forward):
                eng.reg_mov(last, step)
                with eng.Fori(step, NB, stride):
                    run_event(attention, feed_forward)
                    eng.reg_alu(stride, step, last, op=ALU.subtract)
                    eng.reg_mov(last, step)

            return load_next, run, sections

        @block.sync
        def _(sp):
            sp.dma_start(x2[0:C], x_half[0]).then_inc(S["x_loaded"], 16)
            sp.dma_start(mean_w[:], mean_mat).then_inc(S["x_loaded"], 16)
            sp.wait_ge(S["w_zeroed"], 1)
            for h in range(2):
                sp.dma_start(wv_bd[C * h:C * h + C, C * h:C * h + C], w_v).then_inc(S["w_loaded"], 16)
            for h in range(2):
                sp.dma_start(wqk[C * h:C * h + C, h, :], w_qk).then_inc(S["w_loaded"], 16)
            sp.dma_start(masks_xy[:], masks).then_inc(S["c_loaded"], 16)
            for b in range(4):
                sp.dma_start(k_aug[C:P, b, :, :], key_onehot).then_inc(S["c_loaded"], 16)
            sp.wait_ge(S["table_ready"], 1)
            sp.dma_start(next_steps, ahead_i[:]).then_inc(S["table_spilled"], 16)
            sp.wait_ge(S["table_spilled"], 16)
            sp.dma_start(table[:], next_steps.rearrange("p n -> (p n)").unsqueeze(0)
                         ).then_inc(S["table_loaded"], 16)

            def attention(a, f, ev, row):
                sp.wait_ge(S["fold_d"], a + 1)
                sp.dma_start(wa[:], attn_pack[bass.ds(row, 1)].rearrange("o c k d -> (o c) k d")
                             ).then_inc(S["aw_loaded"], 16)

            def feed_forward(a, f, ev, row):
                sp.wait_ge(S["ffn_done"], f + 1)
                for h in range(2):
                    sp.dma_start(w1d[C * h:C * h + C, :],
                                 ffn_w1[bass.ds(row, 1)].rearrange("o c k -> (o c) k")
                                 ).then_inc(S["fw_loaded"], 16)
                sp.dma_start(w2p[:], ffn_pack[bass.ds(row, 1)].rearrange("o p k -> (o p) k")
                             ).then_inc(S["fw_loaded"], 16)

            load_next, run, sections = routing(sp)
            load_next()
            run(attention, feed_forward)
            base = sp.snap(4 * sp.snap(sections()))
            for j in range(4):
                sp.wait_ge(S["summed"], base + j + 1)
                sp.sem_inc(S["passed"], 1)
                for h in range(2):
                    sp.dma_start(o_half[h][:, j // 2, (j % 2) * 512:(j % 2) * 512 + 512],
                                 osum[C * h:C * h + C, j * 512:j * 512 + 512]).then_inc(S["stored"], 16)
            sp.wait_ge(S["stored"], 16 * 8)

        @block.gpsimd
        def _(pool):
            nc.gpsimd.memset(ones_c[:], 1.0)
            nc.gpsimd.memset(wqk[:], 0.0)
            nc.gpsimd.memset(wv_bd[:], 0.0).then_inc(S["w_zeroed"], 1)
            nc.gpsimd.memset(gx[:], 0.0)
            nc.gpsimd.memset(gy[:], 0.0)
            nc.gpsimd.memset(k_aug[0:C], 0.0)
            nc.gpsimd.memset(v_pad[:], 0.0)
            nc.gpsimd.memset(v_st[:], 0.0)
            nc.gpsimd.memset(prob[:], 0.0)
            nc.gpsimd.memset(qk_bd[:], 0.0)
            nc.gpsimd.memset(vo_bd[:], 0.0).then_inc(S["zeroed"], 1)

            def stage(b2, hb, xb, p, early=False):
                if early:
                    if xb == 0:
                        pool.wait_ge(S["q_copied"], 8)
                        pool.wait_ge(S["v_copied"], 4)
                    pool.wait_ge(S["bias_added"], 6 + 4 * xb)
                else:
                    pool.wait_ge(S["scores_ready"], p - 1)
                for h in range(2):
                    src = q_aug[:, bass.ds(2 * h + b2, 1), bass.ds(BR * hb, BR), BC * xb:BC * xb + BC]
                    ins = nc.gpsimd.tensor_tensor(
                        q_st[:, xb, h, :].rearrange("p (a r c) -> p a r c", a=1, c=BC), src,
                        ones_c[:].unsqueeze(2).unsqueeze(3).broadcast_to([P, 1, BR, BC]), ALU.mult)
                ins.then_inc(S["q_staged"], 1)
                if not early:
                    pool.wait_ge(S["v_turned"], p - 1)
                src = v_pad[:, bass.ds(b2, 1), bass.ds(BR * hb, KR), BC * xb:BC * xb + KC]
                nc.gpsimd.tensor_tensor(
                    v_st[:, xb, 0:NKEY].rearrange("p (a r c) -> p a r c", a=1, c=KC), src,
                    ones_c[:].unsqueeze(2).unsqueeze(3).broadcast_to([P, 1, KR, KC]), ALU.mult
                    ).then_inc(S["v_staged"], 1)

            for xb in range(2):
                stage(0, 0, xb, xb, early=True)
            pool.wait_ge(S["bias_added"], 12)
            for xb in range(2):
                stage(0, 1, xb, 2 + xb)
            pool.wait_ge(S["bias_added"], 16)
            with pool.Fori(2, 8) as r:
                b2 = pool.snap(r // 4)
                hb = pool.snap(r % 4)
                for xb in range(2):
                    stage(b2, hb, xb, 2 * r + xb)

            def add_up(j):
                s = slice(j * 512, j * 512 + 512)
                nc.gpsimd.tensor_tensor(osum[:, s], x2f[:, s], h2[:, s], ALU.add
                                        ).then_inc(S["summed"], 1)

            load_next, run, sections = routing(pool)
            load_next()
            for j in range(4):
                pool.wait_ge(S["normed"], 4 + j + 1)
                add_up(j)

            def attention(a, f, ev, row):
                for j in range(4):
                    pool.wait_ge(S["a_stored"], 4 * a + j + 1)
                    pool.sem_inc(S["passed"], 1)
                    add_up(j)

            def feed_forward(a, f, ev, row):
                for j in range(4):
                    pool.wait_ge(S["z_ready"], 4 * f + j + 1)
                    pool.sem_inc(S["passed"], 1)
                    add_up(j)

            run(attention, feed_forward)

        @block.tensor
        def _(pe):
            def norm(src, k, between=None):
                for j in range(4):
                    nc.tensor.matmul(ps[:, j, :], mean_w[:, 0:P], src[:, j * 512:j * 512 + 512],
                                     start=True, stop=True).then_inc(S["mean_ready"], 1)
                for j in range(4):
                    pe.wait_ge(S["squared"], 4 * k + j + 1)
                    for slot in range(2):
                        s0 = (2 * j + slot) * 256
                        mm = nc.tensor.matmul(ps[32 * j:32 * j + 32, 4, 0:256],
                                              mean_w[:, P + 32 * slot:P + 32 * slot + 32],
                                              sq[:, s0:s0 + 256], start=(slot == 0), stop=(slot == 1))
                mm.then_inc(S["var_ready"], 1)
                if between is not None:
                    between()
                pe.wait_ge(S["s_loaded"], 16)
                pe.wait_ge(S["inv_ready"], k + 1)
                for j in range(4):
                    for slot in range(2):
                        mm = nc.tensor.matmul(ps[:, j, 256 * slot:256 * slot + 256],
                                              spread_w[:, 2 * j + slot, :], sq[:, 0:256],
                                              start=True, stop=True)
                    mm.then_inc(S["spread_ready"], 1)

            pe.wait_ge(S["x_loaded"], 48)
            norm(x2f, 0)

            pe.wait_ge(S["w_loaded"], 96)
            for j in range(4):
                pe.wait_ge(S["normed"], j + 1)
                nc.tensor.matmul(ps[:, VBANK[j], :], wv_bd[:], h2[:, j * 512:j * 512 + 512],
                                 start=True, stop=True).then_inc(S["v_ready"], 1)
                if j == 0:
                    for h in range(2):
                        mm = nc.tensor.matmul(ps[C * h:C * h + C, 7, 0:TX + TY], wq_nat[:], rel_tab[:],
                                              start=True, stop=True)
                    mm.then_inc(S["tab_ready"], 1)
            for j in range(4):
                for h in range(2):
                    k = 2 * j + h
                    if k == 3:
                        pe.wait_ge(S["tab_copied"], 4)
                    if k > 3:
                        pe.wait_ge(S["v_copied"], k - 3)
                    nc.tensor.matmul(ps[:, QKBANK[k], :], wqk[:, h, :], h2[:, j * 512:j * 512 + 512],
                                     start=True, stop=True).then_inc(S["qk_ready"], 1)
            h4 = h2.rearrange("p (a h w) -> p a h w", a=2, w=WW)
            for w in range(WW):
                k, cols = w // 8, slice(w % 8 * 64, w % 8 * 64 + 64)
                if w % 8 == 0:
                    pe.wait_ge(S["q_copied"], QKBANK.index(BBANK[k]) + 1)
                    pe.wait_ge(S["k_copied"], QKBANK.index(BBANK[k]) + 1)
                nc.tensor.matmul(ps[0:C, BBANK[k], cols], gx[:, (-w) % KC, :, :].rearrange("p a r -> p (a r)"),
                                 h4[:, :, :, w], start=True, stop=True)
                mm = nc.tensor.matmul(ps[C:P, BBANK[k], cols],
                                      gy[:, (-w) % KR, :, :].rearrange("p a r -> p (a r)"),
                                      h4[:, :, w, :], start=True, stop=True)
                if w % 8 == 7:
                    mm.then_inc(S["bias_ready"], 1)

            def scores(b2, hb, xb, p, early=False):
                pe.wait_ge(S["q_staged"], p + 1)
                if not early:
                    pe.wait_ge(S["exp_done"], p - 1)
                for h in range(2):
                    mm = nc.tensor.matmul(
                        ps[:, 2 * xb + h, 0:NKEY], q_st[:, xb, h, :],
                        k_aug[:, bass.ds(2 * h + b2, 1), bass.ds(BR * hb, KR), BC * xb:BC * xb + KC],
                        start=True, stop=True)
                mm.then_inc(S["scores_ready"], 1)

            def turn_values(pp, p, first=False):
                pe.wait_ge(S["v_staged"], p + 1)
                if not first:
                    pe.wait_ge(S["vk_copied"], p)
                for c in range(NCH):
                    mm = nc.tensor.transpose(ps[0:CH, 6, c * P:c * P + P],
                                             v_st[:, pp, c * CH:c * CH + CH], eye[:])
                mm.then_inc(S["v_turned"], 1)

            def turn_probs(pp, p, first=False):
                pe.wait_ge(S["probs_ready"], p + 1)
                if not first:
                    pe.wait_ge(S["pt_copied"], p)
                for h in range(2):
                    for c in range(NCH):
                        mm = nc.tensor.transpose(ps[0:CH, 4 + h, c * P:c * P + P],
                                                 prob[:, pp, h, c * CH:c * CH + CH], eye[:])
                mm.then_inc(S["probs_turned"], 1)

            def mix(pp, p, first=False):
                pe.wait_ge(S["pt_copied"], p + 1)
                pe.wait_ge(S["vk_copied"], p + 1)
                if not first:
                    pe.wait_ge(S["mixed"], p)
                for c in range(NCH):
                    for h in range(2):
                        mm = nc.tensor.matmul(ps[C * h:C * h + C, 7, 0:P],
                                              v_key[0:CH, pp, c, C * h:C * h + C],
                                              prob_t[0:CH, pp, h, c, :],
                                              start=(c == 0), stop=(c == NCH - 1))
                mm.then_inc(S["pv_done"], 1)

            pe.wait_ge(S["c_loaded"], 16 * 6)
            scores(0, 0, 0, 0, early=True)
            scores(0, 0, 1, 1, early=True)
            pe.wait_ge(S["bias_added"], 12)
            turn_probs(0, 0, first=True)
            pe.wait_ge(S["bias_added"], 16)
            turn_values(0, 0, first=True)

            def rest_of_first(b2, hb):
                scores(b2, hb, 0, 2)
                turn_values(1, 1)
                mix(0, 0, first=True)
                turn_probs(1, 1)
                scores(b2, hb, 1, 3)
                turn_values(0, 2)
                mix(1, 1)

            rest_of_first(0, 1)
            with pe.Fori(2, 8) as r:
                b2 = pe.snap(r // 4)
                hb = pe.snap(r % 4)
                for xb in range(2):
                    p = 2 * r + xb - 2
                    turn_probs(xb, p)
                    scores(b2, hb, xb, p + 2)
                    turn_values(1 - xb, p + 1)
                    mix(xb, p)
            turn_probs(0, 14)
            turn_values(1, 15)
            mix(0, 14)
            turn_probs(1, 15)
            mix(1, 15)

            def turn_row(bank, src=h2):
                nc.tensor.transpose(ps[0:1, bank, 0:P], src[:, 0:1], eye[:]).then_inc(S["row_turned"], 1)

            pe.wait_ge(S["mixed"], NPAIR)
            turn_row(7, x2f)
            load_next, run, sections = routing(pe)
            norm(x2f, 1, between=load_next)

            def attention(a, f, ev, row):
                pe.wait_ge(S["normed"], 8)
                pe.wait_ge(S["aw_loaded"], 16 * (a + 1))
                pe.sem_inc(S["passed"], 1)
                for h in range(2):
                    nc.tensor.matmul(ps[C * h:C * h + C, 0, 0:C], wa[:, 0, :], wa[:, 1, :],
                                     start=True, stop=True)
                    mm = nc.tensor.matmul(ps[C * h:C * h + C, 1, 0:C], wa[:, 2, :], wa[:, 3, :],
                                          start=True, stop=True)
                mm.then_inc(S["fold_ready"], 1)
                base = pe.snap(NT * a)
                parts = pe.snap(16 * pe.snap(a + f))

                def queries(b2, c):
                    if (b2, c) == (1, 1):
                        pe.wait_ge(S["g_low"], 8 * a + 4)
                    s0 = b2 * NPOS + c * 512
                    nc.tensor.matmul(ps[:, GBANK[2 * b2 + c], :], qk_bd[:], h2[:, s0:s0 + 512],
                                     start=True, stop=True).then_inc(S["g_ready"], 1)

                def values(b2):
                    bank = 4 + 2 * b2
                    if b2 == 1:
                        pe.wait_ge(S["g_low"], 8 * a + 8)
                    for c in range(NKC):
                        s0 = b2 * NPOS + c * P
                        mm = nc.tensor.matmul(ps[:, bank + c // 4, (c % 4) * P:(c % 4) * P + P],
                                              h2[:, s0:s0 + P], vo_bd[:], start=True, stop=True)
                    mm.then_inc(S["vo_ready"], 1)

                def tile_scores(n):
                    b2, q0, h = n // NTILE, (n % NTILE) // 2 * P, n % 2
                    if n % 8 < 2:
                        pe.wait_ge(S["g_low"], 8 * a + 2 * (n // 8) + h + 1)
                    if n % NTILE < 2:
                        pe.wait_ge(S["high_low_act"], parts + 4 * (2 * b2 + 1) + 3 + h)
                    if n >= 2:
                        pe.wait_ge(S["s_exp"], base + n - 1)
                    for c in range(2):
                        for part in range(2):
                            mm = nc.tensor.matmul(ps[:, 2 * h + c, :], g_st[:, b2, h, q0:q0 + P],
                                                  h_st[:, b2, h, part, c * 512:c * 512 + 512],
                                                  start=(part == 0), stop=(part == 1))
                    mm.then_inc(S["s_ready"], 1)

                def tile_turn(n):
                    pe.wait_ge(S["s_prob"], base + n + 1)
                    if n == 0:
                        pe.wait_ge(S["vo_copied"], 2 * a + 1)
                    else:
                        pe.wait_ge(S["s_pt"], base + n)
                    for c in range(NKC):
                        mm = nc.tensor.transpose(ps[:, 4 + c // 4, (c % 4) * P:(c % 4) * P + P],
                                                 pr[:, n % 2, c * P:c * P + P], eye[:])
                    mm.then_inc(S["s_turned"], 1)

                def mix_chunk(g, c):
                    if c == 0:
                        pe.wait_ge(S["s_pt"], base + 8 * g + 8)
                        if g < 2:
                            pe.wait_ge(S["vo_copied"], 2 * a + 2)
                        else:
                            pe.wait_ge(S["a_stored"], 4 * a + g - 1)
                            if g == 2:
                                pe.wait_ge(S["decided"], a + f + 2)
                    for h in range(2):
                        mm = nc.tensor.matmul(ps[C * h:C * h + C, 6 + g % 2, :],
                                              vk[:, g // 2, c, C * h:C * h + C], prt[:, g % 2, h, c, :],
                                              start=(c == 0), stop=(c == NKC - 1))
                    if c == NKC - 1:
                        mm.then_inc(S["s_pv"], 1)

                pe.wait_ge(S["fold_a"], a + 1)
                pe.wait_ge(S["high_low_dve"], parts + 8)
                queries(0, 0)
                pe.wait_ge(S["fold_d"], a + 2)
                pe.wait_ge(S["section_done"], a + f + 1)
                values(0)
                tile_scores(0)
                tile_scores(1)
                for n in range(NT):
                    if n + 2 < NT:
                        tile_scores(n + 2)
                    tile_turn(n)
                    if n == 0:
                        queries(0, 1)
                        queries(1, 0)
                    if n == 3:
                        queries(1, 1)
                    if n == 6:
                        values(1)
                    if n >= 8:
                        mix_chunk(n // 8 - 1, n % 8)
                    if n == 18:
                        pe.wait_ge(S["a_stored"], 4 * a + 1)
                        turn_row(6)
                for c in range(NKC):
                    mix_chunk(3, c)

            def feed_forward(a, f, ev, row):
                pe.wait_ge(S["normed"], 8)
                pe.wait_ge(S["w1_act"], f + 1)
                pe.wait_ge(S["w1_dve"], 2 * f + 2)
                parts = pe.snap(16 * pe.snap(a + f))

                def up(t):
                    b2, s0 = t // 2, t % 2 * 512
                    for h in range(2):
                        pe.wait_ge(S["high_low_act"], parts + 4 * t + 3 + h)
                        if t > 0:
                            pe.wait_ge(S["relu_act"], 8 * f + 2 * t - 1 + h)
                            pe.wait_ge(S["relu_dve"], 8 * f + 2 * t - 1 + h)
                        for c in range(2):
                            for part in range(2):
                                mm = nc.tensor.matmul(ps[:, 2 * h + c, :], w1_st[:, c * P:c * P + P],
                                                      h_st[:, b2, h, part, s0:s0 + 512],
                                                      start=(part == 0), stop=(part == 1))
                        mm.then_inc(S["hid_ready"], 1)

                def down(t):
                    pe.wait_ge(S["relu_act"], 8 * f + 2 * t + 2)
                    pe.wait_ge(S["relu_dve"], 8 * f + 2 * t + 2)
                    src = hid if t % 2 == 0 else hid2
                    for c in range(2):
                        for h in range(2):
                            mm = nc.tensor.matmul(ps[C * h:C * h + C, 4 + t % 3, :],
                                                  w2p[:, c * C:c * C + C], src[:, 2 * h + c, :],
                                                  start=(c == 0), stop=(c == 1))
                    mm.then_inc(S["hid_down"], 1)

                up(0)
                up(1)
                pe.wait_ge(S["section_done"], a + f + 1)
                down(0)
                up(2)
                down(1)
                pe.wait_ge(S["z_ready"], 4 * f + 1)
                turn_row(7)
                up(3)
                down(2)
                down(3)

            run(attention, feed_forward)

        @block.scalar
        def _(act):
            def load_table(func):
                nc.scalar.activation(spare[:, 0:1], eps_c[:, 0:1], func)

            def norm(k):
                for j in range(4):
                    act.wait_ge(S["centered"], 4 * k + j + 1)
                    nc.scalar.activation(sq[:, j * 512:j * 512 + 512], xc[:, j * 512:j * 512 + 512],
                                         ACT.Square).then_inc(S["squared"], 1)
                act.wait_ge(S["var_ready"], k + 1)
                nc.scalar.activation(sq[:, 0:256], ps[:, 4, 0:256], ACT.Sqrt,
                                     bias=eps_c[:, k:k + 1]).then_inc(S["std_ready"], 1)

            act.dma_start(x2[C:P], x_half[1]).then_inc(S["x_loaded"], 16)
            act.dma_start(spread_w[:], spread_mat).then_inc(S["s_loaded"], 16)
            act.dma_start(wq_nat[:], w_q).then_inc(S["w_loaded"], 16)
            act.dma_start(rel_tab[:], bias_tables).then_inc(S["w_loaded"], 16)
            act.dma_start(masks8[:, 0, :], attn_mask).then_inc(S["m_loaded"], 16)
            act.dma_start(masks8[:, 1, :], ffn_mask).then_inc(S["m_loaded"], 16)
            act.dma_start(iota[:], iotas).then_inc(S["m_loaded"], 16)
            act.dma_start(eye[:], ident).then_inc(S["c_loaded"], 16)
            act.wait_ge(S["eps_set"], 1)
            load_table(ACT.Sqrt)
            norm(0)
            act.wait_ge(S["zeroed"], 1)
            for h in range(2):
                act.wait_ge(S["tab_ready"], 1)
                for tab, at, n in ((gx, 0, KC), (gy, TX, KR)):
                    src = ps[C * h:C * h + C, 7, at:at + 1]
                    shifted = bass.AP(tensor=src.tensor, offset=src.offset,
                                      ap=[list(src.ap[0]), [1, n], [1, 32]])
                    nc.scalar.copy(tab[C * h:C * h + C, :, h, :], shifted
                                   ).then_inc(S["tab_copied"], 1)
            for j in range(4):
                act.wait_ge(S["v_ready"], j + 1)
                r0 = PAD + 16 * (j % 2)
                nc.scalar.copy(v_pad[:, j // 2, r0:r0 + 16, PAD:PAD + WW],
                               ps[:, VBANK[j], :].rearrange("p (r w) -> p r w", w=WW)
                               ).then_inc(S["v_copied"], 1)
            for j in range(4):
                for h in range(2):
                    act.wait_ge(S["qk_ready"], 2 * j + h + 1)
                    nc.scalar.copy(q_aug[0:C, 2 * h + j // 2, 16 * (j % 2):16 * (j % 2) + 16, :],
                                   ps[0:C, QKBANK[2 * j + h], :].rearrange("p (r w) -> p r w", w=WW)
                                   ).then_inc(S["q_copied"], 1)
            def exps(pp, p, early=False):
                act.wait_ge(S["negmax_ready"], p + 1)
                if not early:
                    act.wait_ge(S["probs_turned"], p - 1)
                for h in range(2):
                    ins = nc.scalar.activation(prob[:, pp, h, 0:NKEY], ps[:, 2 * pp + h, 0:NKEY],
                                               ACT.Exp, bias=negmax[:, pp, h:h + 1],
                                               accum_out=rowsum[:, pp, h:h + 1])
                ins.then_inc(S["exp_done"], 1)

            def copy_turned(pp, p, early=False):
                act.wait_ge(S["probs_turned"], p + 1)
                if not early:
                    act.wait_ge(S["pv_done"], p - 1)
                for h in range(2):
                    ins = nc.scalar.copy(prob_t[0:CH, pp, h, :, :],
                                         ps[0:CH, 4 + h, 0:NCH * P].rearrange("p (c q) -> p c q", c=NCH))
                ins.then_inc(S["pt_copied"], 1)

            exps(0, 0, early=True)
            exps(1, 1, early=True)
            for pp in range(2):
                copy_turned(pp, pp, early=True)
                exps(pp, pp + 2)
            with act.Fori(1, 7) as r:
                for pp in range(2):
                    copy_turned(pp, 2 * r + pp)
                    exps(pp, 2 * r + pp + 2)
            for pp in range(2):
                copy_turned(pp, 14 + pp)

            load_table(ACT.Sqrt)
            norm(1)
            load_table(ACT.Exp)

            def high(t, h):
                rows = slice(C * h, C * h + C)
                nc.scalar.copy(h_st[rows, t // 2, h, 0, t % 2 * 512:t % 2 * 512 + 512],
                               h2[rows, t * 512:t * 512 + 512]).then_inc(S["high_low_act"], 1)

            def low(parts, t, h):
                act.wait_ge(S["high_low_dve"], parts + 4 * t + 2 + 2 * h)
                s = slice(t % 2 * 512, t % 2 * 512 + 512)
                nc.scalar.copy(h_st[C * (1 - h):C * (1 - h) + C, t // 2, h, 1, s],
                               h_f[C * h:C * h + C, t // 2, h, 1, s]).then_inc(S["high_low_act"], 1)

            load_next, run, sections = routing(act)
            load_next()
            for t in range(2):
                act.wait_ge(S["normed"], 4 + t + 1)
                high(t, 0)
                high(t, 1)
                low(0, t, 0)
                low(0, t, 1)

            def attention(a, f, ev, row):
                base = act.snap(NT * a)
                parts = act.snap(16 * act.snap(a + f))

                def query_high(b2, c, h):
                    act.wait_ge(S["g_ready"], 4 * a + 2 * b2 + c + 1)
                    nc.scalar.copy(g_st[C * h:C * h + C, b2, h, c * 512:c * 512 + 512],
                                   ps[C * h:C * h + C, GBANK[2 * b2 + c], :]
                                   ).then_inc(S["g_high"], 1)

                def copy_values(b2):
                    act.wait_ge(S["vo_ready"], 2 * a + b2 + 1)
                    nc.scalar.copy(vk[:, b2, :, :],
                                   ps[:, 4 + 2 * b2:6 + 2 * b2, :].rearrange("p b (c d) -> p (b c) d", c=4)
                                   ).then_inc(S["vo_copied"], 1)

                def exps(n):
                    act.wait_ge(S["s_negmax"], base + n + 1)
                    if n >= 2:
                        act.wait_ge(S["s_turned"], base + n - 1)
                    nc.scalar.activation(pr[:, n % 2, :], ps[:, 2 * (n % 2):2 * (n % 2) + 2, :],
                                         ACT.Exp, bias=negmax[:, 0, n % 2:n % 2 + 1],
                                         accum_out=rowsum[:, 0, n % 2:n % 2 + 1]
                                         ).then_inc(S["s_exp"], 1)

                act.wait_ge(S["fold_ready"], a + 1)
                for h in range(2):
                    ins = nc.scalar.mul(qk_bd[C * h:C * h + C, C * h:C * h + C],
                                        ps[C * h:C * h + C, 0, 0:C], SCALE)
                ins.then_inc(S["fold_a"], 1)
                query_high(0, 0, 0)
                query_high(0, 0, 1)
                exps(0)
                copy_values(0)

                def next_high(t, h):
                    act.wait_ge(S["a_stored"], 4 * a + t + 1)
                    high(t, h)

                between = {1: lambda: (query_high(0, 1, 0), query_high(0, 1, 1)),
                           2: lambda: (query_high(1, 0, 0), query_high(1, 0, 1)),
                           3: lambda: high(2, 0),
                           4: lambda: (query_high(1, 1, 0), query_high(1, 1, 1)),
                           5: lambda: high(2, 1), 7: lambda: copy_values(1),
                           8: lambda: low(parts, 2, 0), 9: lambda: low(parts, 2, 1),
                           10: lambda: (high(3, 0), high(3, 1)),
                           12: lambda: low(parts, 3, 0), 13: lambda: low(parts, 3, 1),
                           18: lambda: next_high(0, 0), 19: lambda: next_high(0, 1),
                           20: lambda: low(parts + 16, 0, 0), 21: lambda: low(parts + 16, 0, 1),
                           26: lambda: next_high(1, 0), 27: lambda: next_high(1, 1),
                           28: lambda: low(parts + 16, 1, 0), 29: lambda: low(parts + 16, 1, 1)}
                for n in range(NT):
                    if n + 1 < NT:
                        exps(n + 1)
                    act.wait_ge(S["s_turned"], base + n + 1)
                    if n % 8 == 0 and n >= 16:
                        act.wait_ge(S["s_pv"], 4 * a + n // 8 - 1)
                    q0 = (n // 2 % 4) * P
                    nc.scalar.copy(prt[:, n // 8 % 2, n % 2, :, q0:q0 + P],
                                   ps[:, 4:6, :].rearrange("p b (c q) -> p (b c) q", c=4)
                                   ).then_inc(S["s_pt"], 1)
                    if n in between:
                        between[n]()

            def feed_forward(a, f, ev, row):
                act.wait_ge(S["normed"], 8)
                act.wait_ge(S["fw_loaded"], 48 * (f + 1))
                nc.scalar.copy(w1_st[0:C, :], w1d[0:C, :]).then_inc(S["w1_act"], 1)
                parts = act.snap(16 * act.snap(a + f))

                def relu(t, h):
                    dst = hid if t % 2 == 0 else hid2
                    act.wait_ge(S["hid_ready"], 8 * f + 2 * t + h + 1)
                    if t >= 2:
                        act.wait_ge(S["hid_down"], 4 * f + t - 1)
                    nc.scalar.activation(dst[:, 2 * h, :], ps[:, 2 * h, :], ACT.Relu,
                                         bias=w2p[:, 2 * C:2 * C + 1]).then_inc(S["relu_act"], 1)

                for t in range(2):
                    relu(t, 0)
                    if t == 0:
                        act.wait_ge(S["section_done"], a + f + 1)
                    high(t + 2, 0)
                    high(t + 2, 1)
                    low(parts, t + 2, 0)
                    relu(t, 1)
                    low(parts, t + 2, 1)
                for t in range(2):
                    relu(t + 2, 0)
                    relu(t + 2, 1)
                    act.wait_ge(S["z_ready"], 4 * f + t + 1)
                    high(t, 0)
                    high(t, 1)
                    low(parts + 16, t, 0)
                    low(parts + 16, t, 1)

            run(attention, feed_forward)

        @block.vector
        def _(dve):
            nc.vector.memset(eps_c[:, 0:1], LN_C_EPS)
            nc.vector.memset(eps_c[:, 1:2], LN_T_EPS).then_inc(S["eps_set"], 1)
            dve.sem_inc(S["fold_d"], 1)
            dve.sem_inc(S["ffn_done"], 1)
            dve.wait_ge(S["x_loaded"], 48)

            def make_table():
                steps = [0]

                def step(ins):
                    steps[0] += 1
                    ins.then_inc(S["dve_step"], 1)
                    dve.wait_ge(S["dve_step"], steps[0])

                dve.wait_ge(S["m_loaded"], 48)
                step(nc.vector.memset(ahead[:], 4.0 * NB))
                step(nc.vector.tensor_copy(kinds[:], masks8[:]))
                step(nc.vector.scalar_tensor_tensor(kinds[:, 0, :], kinds[:, 1, :], 2.0, kinds[:, 0, :],
                                                    ALU.mult, ALU.add))
                step(nc.vector.tensor_scalar(kinds[:, 1, :], kinds[:, 0, :], 0.0, 4.0 * NB,
                                             ALU.is_equal, ALU.mult))
                step(nc.vector.tensor_tensor(kinds[:, 0, :], kinds[:, 0, :], iota[:], ALU.add))
                step(nc.vector.tensor_tensor(ahead[:, 0, 0:NB], kinds[:, 0, :], kinds[:, 1, :], ALU.max))
                by, at = 1, 0
                while by < NB:
                    step(nc.vector.tensor_tensor(ahead[:, 1 - at, 0:NB], ahead[:, at, 0:NB],
                                                 ahead[:, at, by:by + NB], ALU.min))
                    by, at = 2 * by, 1 - at
                nc.vector.tensor_copy(ahead_i[:], ahead[:, at, 0:NB + 1]).then_inc(S["table_ready"], 1)

            def norm(src, k, between=None, after=None):
                for j in range(4):
                    s = slice(j * 512, j * 512 + 512)
                    dve.wait_ge(S["mean_ready"], 4 * k + j + 1)
                    nc.vector.tensor_tensor(xc[:, s], src[:, s], ps[:, j, :], ALU.subtract
                                            ).then_inc(S["centered"], 1)
                if between is not None:
                    between()
                dve.wait_ge(S["std_ready"], k + 1)
                nc.vector.reciprocal(sq[:, 0:256], sq[:, 0:256]).then_inc(S["inv_ready"], 1)
                for j in range(4):
                    s = slice(j * 512, j * 512 + 512)
                    dve.wait_ge(S["spread_ready"], 4 * k + j + 1)
                    nc.vector.tensor_tensor(h2[:, s], xc[:, s], ps[:, j, :], ALU.mult
                                            ).then_inc(S["normed"], 1)
                    if after is not None:
                        after(j)

            norm(x2f, 0, make_table)
            dve.wait_ge(S["zeroed"], 1)
            for j in range(4):
                for h in range(2):
                    dve.wait_ge(S["qk_ready"], 2 * j + h + 1)
                    r0 = PAD + 16 * (j % 2)
                    nc.vector.tensor_copy(k_aug[0:C, 2 * h + j // 2, r0:r0 + 16, PAD:PAD + WW],
                                          ps[C:P, QKBANK[2 * j + h], :].rearrange("p (r w) -> p r w", w=WW)
                                          ).then_inc(S["k_copied"], 1)
            dve.wait_ge(S["c_loaded"], 16 * 6)
            def add_bias(k, by_row):
                dve.wait_ge(S["bias_ready"], k + 1)
                for h in range(2):
                    at = C * by_row + 32 * h
                    if not by_row:
                        dst = q_aug[XROW:XROW + 32, 2 * h:2 * h + 2, :, 8 * k:8 * k + 8].rearrange(
                            "p a r w -> p w a r")
                    else:
                        dst = q_aug[YROW:YROW + 32, 2 * h:2 * h + 2, 8 * k:8 * k + 8, :].rearrange(
                            "p a r w -> p r a w")
                    nc.vector.tensor_tensor(
                        dst, ps[at:at + 32, BBANK[k], :].rearrange("p (w a r) -> p w a r", w=8, a=2),
                        masks_xy[at:at + 32, 8 * k:8 * k + 8].unsqueeze(2).unsqueeze(3)
                        .broadcast_to([32, 8, 2, HH]), ALU.add).then_inc(S["bias_added"], 1)

            for k, by_row in ((0, 0), (0, 1), (1, 0), (2, 0), (3, 0)):
                add_bias(k, by_row)

            def maxima(pp, p):
                dve.wait_ge(S["scores_ready"], p + 1)
                nc.vector.tensor_reduce(negmax[:, pp, :], ps[:, 2 * pp:2 * pp + 2, 0:NKEY], X, ALU.max,
                                        negate=True).then_inc(S["negmax_ready"], 1)

            def normalise(pp, p):
                dve.wait_ge(S["exp_done"], p + 1)
                nc.vector.reciprocal(rinv[:, pp, :], rowsum[:, pp, :]).then_inc(S["rinv_ready"], 1)
                dve.wait_ge(S["rinv_ready"], p + 1)
                for h in range(2):
                    ins = nc.vector.tensor_scalar(prob[:, pp, h, 0:NKEY], prob[:, pp, h, 0:NKEY],
                                                  rinv[:, pp, h:h + 1], None, ALU.mult)
                ins.then_inc(S["probs_ready"], 1)

            def copy_values(pp, p, early=False):
                dve.wait_ge(S["v_turned"], p + 1)
                if not early:
                    dve.wait_ge(S["pv_done"], p - 1)
                nc.vector.tensor_copy(v_key[0:CH, pp, :, :],
                                      ps[0:CH, 6, 0:NCH * P].rearrange("p (c d) -> p c d", c=NCH)
                                      ).then_inc(S["vk_copied"], 1)

            def add_mixed(b2, hb, xb, p):
                dve.wait_ge(S["pv_done"], p + 1)
                win = x2[:, bass.ds(b2, 1), bass.ds(BR * hb, BR), BC * xb:BC * xb + BC]
                nc.vector.tensor_tensor(win, win,
                                        ps[:, 7, 0:P].rearrange("p (a r c) -> p a r c", a=1, c=BC),
                                        ALU.add).then_inc(S["mixed"], 1)

            maxima(0, 0)
            add_bias(1, 1)
            maxima(1, 1)
            normalise(0, 0)
            add_bias(2, 1)
            add_bias(3, 1)
            copy_values(0, 0, early=True)
            normalise(1, 1)
            maxima(0, 2)
            copy_values(1, 1, early=True)
            add_mixed(0, 0, 0, 0)
            normalise(0, 2)
            maxima(1, 3)
            copy_values(0, 2)
            add_mixed(0, 0, 1, 1)
            with dve.Fori(1, 7) as r:
                b2 = dve.snap(r // 4)
                hb = dve.snap(r % 4)
                for xb in range(2):
                    p = 2 * r + xb
                    normalise(1 - xb, p + 1)
                    maxima(xb, p + 2)
                    copy_values(1 - xb, p + 1)
                    add_mixed(b2, hb, xb, p)
            normalise(1, 15)
            copy_values(1, 15)
            add_mixed(1, 3, 0, 14)
            add_mixed(1, 3, 1, 15)
            dve.wait_ge(S["mixed"], NPAIR)

            def decide(n, bank, ev=None):
                dve.wait_ge(S["row_turned"], n + 1)
                if ev is not None:
                    dve.wait_ge(S["info_read"], readers * ev + readers)
                dve.sem_inc(S["passed"], 1)
                nc.vector.max(top8[:], ps[0:1, bank, 0:NOPS]).then_inc(S["op_max"], 1)
                dve.wait_ge(S["op_max"], n + 1)
                dve.sem_inc(S["passed"], 1)
                nc.vector.max_index(idx8[:], top8[:], ps[0:1, bank, 0:NOPS]).then_inc(S["decided"], 1)

            def high_low(parts, t, h):
                rows = slice(C * h, C * h + C)
                s, cols = slice(t % 2 * 512, t % 2 * 512 + 512), slice(t * 512, t * 512 + 512)
                nc.vector.tensor_copy(h_st[C * (1 - h):C * (1 - h) + C, t // 2, h, 0, s],
                                      h2[rows, cols]).then_inc(S["high_low_dve"], 1)
                dve.wait_ge(S["high_low_act"], parts + 4 * t + 1 + h)
                nc.vector.tensor_tensor(h_st[rows, t // 2, h, 1, s], h2[rows, cols],
                                        h_f[rows, t // 2, h, 0, s], ALU.subtract
                                        ).then_inc(S["high_low_dve"], 1)

            def first_parts(j):
                if j < 2:
                    dve.wait_ge(S["normed"], 5)
                    high_low(0, 0, j)

            decide(0, 7)
            load_next, run, sections = routing(dve)
            norm(x2f, 1, between=load_next, after=first_parts)
            dve.wait_ge(S["normed"], 8)
            dve.sem_inc(S["section_done"], 1)
            high_low(0, 1, 0)
            high_low(0, 1, 1)

            def attention(a, f, ev, row):
                base = dve.snap(NT * a)

                parts = dve.snap(16 * dve.snap(a + f))

                def query_low(b2, c, h):
                    dve.wait_ge(S["g_high"], 8 * a + 4 * b2 + 2 * c + h + 1)
                    s = slice(c * 512, c * 512 + 512)
                    nc.vector.tensor_tensor(g_st[C * (1 - h):C * (1 - h) + C, b2, h, s],
                                            ps[C * h:C * h + C, GBANK[2 * b2 + c], :],
                                            g_f[C * h:C * h + C, b2, h, s], ALU.subtract
                                            ).then_inc(S["g_low"], 1)

                def maxima(n):
                    dve.wait_ge(S["s_ready"], base + n + 1)
                    nc.vector.tensor_reduce(negmax[:, 0, n % 2:n % 2 + 1],
                                            ps[:, 2 * (n % 2):2 * (n % 2) + 2, :],
                                            mybir.AxisListType.XY, ALU.max, negate=True
                                            ).then_inc(S["s_negmax"], 1)

                def normalise(n):
                    dve.wait_ge(S["s_exp"], base + n + 1)
                    nc.vector.reciprocal(rinv[:, 0, n % 2:n % 2 + 1], rowsum[:, 0, n % 2:n % 2 + 1]
                                         ).then_inc(S["s_rinv"], 1)
                    dve.wait_ge(S["s_rinv"], base + n + 1)
                    nc.vector.tensor_scalar(pr[:, n % 2, :], pr[:, n % 2, :],
                                            rinv[:, 0, n % 2:n % 2 + 1], None, ALU.mult
                                            ).then_inc(S["s_prob"], 1)

                def store(g):
                    dve.wait_ge(S["s_pv"], 4 * a + g + 1)
                    dve.wait_ge(S["summed"], 4 * dve.snap(a + f) + g + 1)
                    nc.vector.tensor_copy(h2[:, g * 512:g * 512 + 512], ps[:, 6 + g % 2, :]
                                          ).then_inc(S["a_stored"], 1)

                dve.wait_ge(S["fold_ready"], a + 1)
                for h in range(2):
                    ins = nc.vector.tensor_copy(vo_bd[C * h:C * h + C, C * h:C * h + C],
                                                ps[C * h:C * h + C, 1, 0:C])
                ins.then_inc(S["fold_d"], 1)
                query_low(0, 0, 0)
                query_low(0, 0, 1)
                maxima(0)
                maxima(1)

                def next_high_low(t, h):
                    dve.wait_ge(S["a_stored"], 4 * a + t + 1)
                    high_low(parts + 16, t, h)

                between = {2: lambda: (query_low(0, 1, 0), query_low(0, 1, 1)),
                           3: lambda: (query_low(1, 0, 0), query_low(1, 0, 1)),
                           5: lambda: (query_low(1, 1, 0), query_low(1, 1, 1)),
                           7: lambda: high_low(parts, 2, 0), 8: lambda: high_low(parts, 2, 1),
                           11: lambda: high_low(parts, 3, 0), 12: lambda: high_low(parts, 3, 1),
                           17: lambda: store(0), 18: lambda: decide(a + f + 1, 6, ev),
                           19: lambda: next_high_low(0, 0), 20: lambda: next_high_low(0, 1),
                           25: lambda: store(1),
                           27: lambda: next_high_low(1, 0), 28: lambda: next_high_low(1, 1)}
                for n in range(NT):
                    normalise(n)
                    if n + 2 < NT:
                        maxima(n + 2)
                    if n in between:
                        between[n]()
                store(2)
                store(3)
                dve.wait_ge(S["a_stored"], 4 * a + 4)
                dve.sem_inc(S["section_done"], 1)

            def feed_forward(a, f, ev, row):
                dve.wait_ge(S["fw_loaded"], 48 * (f + 1))
                nc.vector.tensor_copy(w1_hi[C:P, :], w1d[C:P, :]).then_inc(S["w1_dve"], 1)
                dve.wait_ge(S["w1_dve"], 2 * f + 1)
                nc.vector.tensor_tensor(w1_st[C:P, :], w1d[C:P, :], w1_hi[C:P, :].bitcast(F32),
                                        ALU.subtract).then_inc(S["w1_dve"], 1)

                parts = dve.snap(16 * dve.snap(a + f))

                def relu(t, h):
                    dst = hid if t % 2 == 0 else hid2
                    dve.wait_ge(S["hid_ready"], 8 * f + 2 * t + h + 1)
                    nc.vector.tensor_scalar(dst[:, 2 * h + 1, :], ps[:, 2 * h + 1, :],
                                            w2p[:, 2 * C + 1:2 * C + 2], 0.0, ALU.add, ALU.max
                                            ).then_inc(S["relu_dve"], 1)

                def store(t):
                    dve.wait_ge(S["hid_down"], 4 * f + t + 1)
                    dve.wait_ge(S["summed"], 4 * dve.snap(a + f) + t + 1)
                    nc.vector.tensor_scalar(h2[:, t * 512:t * 512 + 512], ps[:, 4 + t % 3, :],
                                            w2p[:, 2 * C + 2:2 * C + 3], None, ALU.add
                                            ).then_inc(S["z_ready"], 1)

                for t in range(4):
                    relu(t, 0)
                    if t < 2:
                        high_low(parts, t + 2, 0)
                    relu(t, 1)
                    if t < 2:
                        high_low(parts, t + 2, 1)
                    if t == 2:
                        decide(a + f + 1, 7, ev)
                    if t > 0:
                        store(t - 1)
                    if t >= 2:
                        dve.wait_ge(S["z_ready"], 4 * f + t - 1)
                        high_low(parts + 16, t - 2, 0)
                        high_low(parts + 16, t - 2, 1)
                store(3)
                dve.wait_ge(S["z_ready"], 4 * f + 4)
                dve.sem_inc(S["ffn_done"], 1)
                dve.sem_inc(S["section_done"], 1)

            run(attention, feed_forward)


def constants():
    import numpy as np

    key_onehot = np.zeros((C, HP, WP), np.float32)
    for r in range(KC):
        key_onehot[r, :, r::KC] = 1.0
    for r in range(KR):
        key_onehot[YROW - XROW + r, r::KR, :] = 1.0
    masks = np.zeros((P, WW), np.float32)
    for h in range(2):
        for r in range(KC):
            for w in range(WW):
                masks[32 * h + r, w] = 0.0 if (r - w) % KC < KS else -1e30
        for r in range(KR):
            for y in range(HH):
                masks[C + 32 * h + r, y] = 0.0 if (r - y) % KR < KS else -1e30
    ident = np.eye(P, dtype=np.float32)
    mean_mat = np.zeros((P, P + 2 * 32), np.float32)
    spread_mat = np.zeros((P, 8, P), np.float32)
    for h in range(2):
        rows = slice(C * h, C * h + C)
        mean_mat[rows, rows] = 1.0 / C
        for slot in range(2):
            at = P + 32 * slot + 16 * slot + 8 * h
            mean_mat[rows, at:at + 8] = 1.0 / C
            for j in range(4):
                spread_mat[32 * j + 16 * slot + 8 * h, 2 * j + slot, rows] = 1.0
    iotas = np.tile(4.0 * np.arange(NB, dtype=np.float32), (NOPS, 1))
    return key_onehot, masks, ident, mean_mat, spread_mat, iotas


def kernel(x, L0_conv_wq, L0_conv_wk, L0_conv_wv, L0_conv_rel_x, L0_conv_rel_y,
           L0_ffn_ffn_w1, L0_ffn_ffn_b1, L0_ffn_ffn_w2, L0_ffn_ffn_b2,
           L0_ffn_wq, L0_ffn_wk, L0_ffn_wv, L0_ffn_wo, L0_ffn_attn_mask, L0_ffn_ffn_mask):
    import numpy as np
    import concourse.bacc as bacc
    from concourse.bass_utils import run_bass_kernel_spmd

    x = np.ascontiguousarray(x)
    wq, wk, wv = (np.asarray(w) for w in (L0_conv_wq, L0_conv_wk, L0_conv_wv))
    rel_x, rel_y = np.asarray(L0_conv_rel_x), np.asarray(L0_conv_rel_y)
    tables = np.zeros((C, TX + TY), np.float32)
    half = rel_x.shape[0]
    for c in range(C):
        d = c % (2 * half)
        table, rel, period, length, at = ((0, rel_x, KC, TX, 0) if d < half else (1, rel_y, KR, TY, TX))
        for t in range(length):
            if t % period < KS:
                tables[c, at + t] = rel[d % half, t % period]
    n = NB * NOPS
    flat = lambda w: np.asarray(w).reshape((n,) + np.asarray(w).shape[2:])
    turned = lambda w: flat(w).transpose(0, 2, 1)
    attn_pack = np.ascontiguousarray(np.stack(
        [turned(L0_ffn_wq), turned(L0_ffn_wk), turned(L0_ffn_wv), flat(L0_ffn_wo)], axis=2))
    w2 = flat(L0_ffn_ffn_w2).reshape(n, 2, P, C).transpose(0, 2, 1, 3).reshape(n, P, 2 * C)
    b1 = flat(L0_ffn_ffn_b1).reshape(n, 2, P).transpose(0, 2, 1)
    b2 = np.concatenate([flat(L0_ffn_ffn_b2)] * 2, axis=1)[:, :, None]
    ffn_pack = np.ascontiguousarray(np.concatenate([w2, b1, b2], axis=2))
    key_onehot, masks, ident, mean_mat, spread_mat, iotas = constants()
    arrays = {
        "x": x,
        "w_qk": np.ascontiguousarray(np.concatenate([wq.T, wk.T], axis=1)),
        "w_q": np.ascontiguousarray(wq),
        "w_v": np.ascontiguousarray(wv.T),
        "bias_tables": tables,
        "key_onehot": key_onehot, "masks": masks, "ident": ident, "mean_mat": mean_mat, "spread_mat": spread_mat,
        "iotas": iotas,
        "attn_mask": np.ascontiguousarray(np.asarray(L0_ffn_attn_mask).T),
        "ffn_mask": np.ascontiguousarray(np.asarray(L0_ffn_ffn_mask).T),
        "attn_pack": attn_pack,
        "ffn_w1": np.ascontiguousarray(flat(L0_ffn_ffn_w1)),
        "ffn_pack": ffn_pack,
    }
    nc = bacc.Bacc("TRN2", target_bir_lowering=False, num_devices=1)
    handles = {k: nc.dram_tensor(f"in_{k}", a.shape, mybir.dt.from_np(a.dtype), kind="ExternalInput").ap()
               for k, a in arrays.items()}
    out = nc.dram_tensor("out", x.shape, F32, kind="ExternalOutput").ap()
    build(nc, out=out, **handles)
    r = run_bass_kernel_spmd(nc, [{f"in_{k}": a for k, a in arrays.items()}], core_ids=[0])
    return r.results[0]["out"]
```
